# Optimizing a Trainium2 kernel written in Bass

```python
import numpy as np
import jax
import jax.numpy as jnp

def _softmax(x, axis=-1):
    return jax.nn.softmax(x, axis=axis)

def _gelu(x):
    return jax.nn.gelu(x, approximate=True)

def _silu(x):
    return jax.nn.silu(x)

def _sigmoid(x):
    return jax.nn.sigmoid(x)

def _layernorm(x, axis=-1, eps=1e-05):
    m = jnp.mean(x, axis=axis, keepdims=True)
    v = jnp.var(x, axis=axis, keepdims=True)
    return (x - m) / jnp.sqrt(v + eps)

def _scatter_add(tgt, idx, src, axis=0):
    return tgt.at[idx].add(src)

def _segment_sum(src, seg, n):
    return jax.ops.segment_sum(src, seg, n)
kernel_name = 'mk_adaln_ffn_d1_seqx_r2_963f40'

def setup_inputs(seed: int=0):
    np.random.seed(seed)
    _w = jnp.asarray

    def _rec_inputs():
        import jax
        import jax.numpy as jnp
        _rk = jax.random.key(seed)
        x = -0.000125 + 0.9999 * jax.random.normal(jax.random.fold_in(_rk, 1), (4, 1024, 1024), jnp.float32)
        _lenS = 1024 - jax.random.randint(jax.random.fold_in(_rk, 7), (4,), 0, max(1, 1024 // 4) + 1, jnp.int32)
        _lenS2 = 1024 - jax.random.randint(jax.random.fold_in(_rk, 8), (4,), 0, max(1, 1024 // 4) + 1, jnp.int32)
        fside_BxSxS_0 = -1.52775e-05 + 0.999936 * jax.random.normal(jax.random.fold_in(_rk, 11), (4, 1024, 1024), jnp.float32)
        cond_512 = -5.03954e-05 + 1.00559 * jax.random.normal(jax.random.fold_in(_rk, 12), (4, 256), jnp.float32)
        return (x, fside_BxSxS_0, cond_512)
    x, fside_BxSxS_0, cond_512 = _rec_inputs()

    def _L0_cond_setup():
        import jax, jax.numpy as jnp
        from jax import lax
        import numpy as np
        B, T, C, TD = (8, 1024, 1024, 256)

        def _bi_wkv(r, k, v, w, u, time_emb):
            tf = jax.nn.sigmoid(jnp.sum(time_emb, axis=-1))[:, None, None]
            decay = jnp.exp(-jnp.exp(w.astype(jnp.float32)))[None, :] * (0.5 + 0.5 * tf[:, :, 0])
            kf = k.astype(jnp.float32)
            vf = v.astype(jnp.float32)
            ek = jnp.exp(jnp.minimum(kf, 30.0))
            ekv = ek * vf

            def step(carry, x):
                a, b = carry
                ekv_t, ek_t = x
                a = a * decay + ekv_t
                b = b * decay + ek_t
                return ((a, b), (a, b))
            ekv_t = jnp.swapaxes(ekv, 0, 1)
            ek_t = jnp.swapaxes(ek, 0, 1)
            init = (jnp.zeros_like(decay), jnp.zeros_like(decay))
            _, (nf, df) = lax.scan(step, init, (ekv_t, ek_t))
            _, (nb, db) = lax.scan(step, init, (ekv_t, ek_t), reverse=True)
            nf = jnp.swapaxes(nf, 0, 1)
            df = jnp.swapaxes(df, 0, 1)
            nb = jnp.swapaxes(nb, 0, 1)
            db = jnp.swapaxes(db, 0, 1)
            euk = jnp.exp(jnp.minimum(u.astype(jnp.float32)[None, None, :] + kf, 30.0))
            num = nf + nb - ekv + euk * vf
            den = df + db - ek + euk
            base = jax.nn.sigmoid(r.astype(jnp.float32)) * (num / jnp.maximum(den, 1e-08))
            out = base * (0.8 + 0.2 * tf)
            return out.astype(r.dtype)
        key = jax.random.key(seed)
        ks = jax.random.split(key, 6)
        return {'r': jax.random.normal(ks[0], (B, T, C), dtype=jnp.float32), 'k': jax.random.normal(ks[1], (B, T, C), dtype=jnp.float32), 'v': jax.random.normal(ks[2], (B, T, C), dtype=jnp.float32), 'w': jax.random.normal(ks[3], (C,), dtype=jnp.float32), 'u': jax.random.normal(ks[4], (C,), dtype=jnp.float32), 'time_emb': jax.random.normal(ks[5], (B, TD), dtype=jnp.float32)}
    _L0_cond_all = _L0_cond_setup()
    _L0_cond_in = {k: v for k, v in _L0_cond_all.items() if k in ('w', 'u')}
    del _L0_cond_all

    def _L0_ffn_setup():
        import jax, jax.numpy as jnp
        import numpy as np
        D_IN = 1024
        D_OUT = 1024
        RANK = 16
        N_EXPERTS = 16
        MAX_EXPERTS = 32
        ROUTER_HID = 64
        TOPK = 2
        ALPHA = 1.0

        def _forward(x, W, bias, rw1, rb1, rw2, rb2, A, B, gates):
            lead = x.shape[:-1]
            x_flat = x.reshape(-1, D_IN)
            n = x_flat.shape[0]
            feat = jax.lax.stop_gradient(x_flat)
            h = jax.nn.silu(feat @ rw1.T + rb1)
            logits = (h @ rw2.T + rb2)[:, :N_EXPERTS] + gates[None, :]
            topv, topi = jax.lax.top_k(logits, TOPK)
            sm = jax.nn.softmax(topv, axis=-1)
            rows = jnp.arange(n)[:, None]
            coeff = jnp.zeros_like(logits).at[rows, topi].set(sm)
            base = x_flat @ W.T + bias
            xa = jnp.einsum('ni,eri->ner', x_flat, A)
            wxa = xa * coeff[:, :, None]
            delta = jnp.einsum('ner,eor->no', wxa, B)
            out = base + ALPHA * delta
            return out.reshape(*lead, D_OUT)
        key = jax.random.key(seed)
        ks = jax.random.split(key, 10)
        s = 0.02
        x = jax.random.normal(ks[0], (4, 2048, D_IN), dtype=jnp.float32)
        W = jax.random.normal(ks[1], (D_OUT, D_IN), dtype=jnp.float32) * s
        bias = jax.random.normal(ks[2], (D_OUT,), dtype=jnp.float32) * s
        rw1 = jax.random.normal(ks[3], (ROUTER_HID, D_IN), dtype=jnp.float32) * s
        rb1 = jnp.zeros((ROUTER_HID,), dtype=jnp.float32)
        rw2 = jax.random.normal(ks[4], (MAX_EXPERTS, ROUTER_HID), dtype=jnp.float32) * s
        rb2 = jnp.zeros((MAX_EXPERTS,), dtype=jnp.float32)
        A = jax.random.normal(ks[5], (N_EXPERTS, RANK, D_IN), dtype=jnp.float32) * s
        B = jax.random.normal(ks[6], (N_EXPERTS, D_OUT, RANK), dtype=jnp.float32) * s
        gates = jnp.ones((N_EXPERTS,), dtype=jnp.float32)
        return {'x': x, 'W': W, 'bias': bias, 'rw1': rw1, 'rb1': rb1, 'rw2': rw2, 'rb2': rb2, 'A': A, 'B': B, 'gates': gates}
    _L0_ffn_all = _L0_ffn_setup()
    _L0_ffn_in = {k: v for k, v in _L0_ffn_all.items() if k in ('W', 'bias', 'rw1', 'rb1', 'rw2', 'rb2', 'A', 'B', 'gates')}
    del _L0_ffn_all
    return {'x': x, 'fside_BxSxS_0': fside_BxSxS_0, 'cond_512': cond_512, 'L0_cond_w': _L0_cond_in['w'], 'L0_cond_u': _L0_cond_in['u'], 'L0_ffn_W': _L0_ffn_in['W'], 'L0_ffn_bias': _L0_ffn_in['bias'], 'L0_ffn_rw1': _L0_ffn_in['rw1'], 'L0_ffn_rb1': _L0_ffn_in['rb1'], 'L0_ffn_rw2': _L0_ffn_in['rw2'], 'L0_ffn_rb2': _L0_ffn_in['rb2'], 'L0_ffn_A': _L0_ffn_in['A'], 'L0_ffn_B': _L0_ffn_in['B'], 'L0_ffn_gates': _L0_ffn_in['gates']}

def reference(x, fside_BxSxS_0, cond_512, L0_cond_w, L0_cond_u, L0_ffn_W, L0_ffn_bias, L0_ffn_rw1, L0_ffn_rb1, L0_ffn_rw2, L0_ffn_rb2, L0_ffn_A, L0_ffn_B, L0_ffn_gates):
    import jax
    import jax.numpy as jnp

    def _L0_cond_ref(r, k, v, w, u, time_emb):
        import jax, jax.numpy as jnp
        from jax import lax
        import numpy as np
        B, T, C, TD = (8, 1024, 1024, 256)

        def _bi_wkv(r, k, v, w, u, time_emb):
            tf = jax.nn.sigmoid(jnp.sum(time_emb, axis=-1))[:, None, None]
            decay = jnp.exp(-jnp.exp(w.astype(jnp.float32)))[None, :] * (0.5 + 0.5 * tf[:, :, 0])
            kf = k.astype(jnp.float32)
            vf = v.astype(jnp.float32)
            ek = jnp.exp(jnp.minimum(kf, 30.0))
            ekv = ek * vf

            def step(carry, x):
                a, b = carry
                ekv_t, ek_t = x
                a = a * decay + ekv_t
                b = b * decay + ek_t
                return ((a, b), (a, b))
            ekv_t = jnp.swapaxes(ekv, 0, 1)
            ek_t = jnp.swapaxes(ek, 0, 1)
            init = (jnp.zeros_like(decay), jnp.zeros_like(decay))
            _, (nf, df) = lax.scan(step, init, (ekv_t, ek_t))
            _, (nb, db) = lax.scan(step, init, (ekv_t, ek_t), reverse=True)
            nf = jnp.swapaxes(nf, 0, 1)
            df = jnp.swapaxes(df, 0, 1)
            nb = jnp.swapaxes(nb, 0, 1)
            db = jnp.swapaxes(db, 0, 1)
            euk = jnp.exp(jnp.minimum(u.astype(jnp.float32)[None, None, :] + kf, 30.0))
            num = nf + nb - ekv + euk * vf
            den = df + db - ek + euk
            base = jax.nn.sigmoid(r.astype(jnp.float32)) * (num / jnp.maximum(den, 1e-08))
            out = base * (0.8 + 0.2 * tf)
            return out.astype(r.dtype)
        return _bi_wkv(r, k, v, w, u, time_emb)

    def _L0_ffn_ref(x, W, bias, rw1, rb1, rw2, rb2, A, B, gates):
        import jax, jax.numpy as jnp
        import numpy as np
        D_IN = 1024
        D_OUT = 1024
        RANK = 16
        N_EXPERTS = 16
        MAX_EXPERTS = 32
        ROUTER_HID = 64
        TOPK = 2
        ALPHA = 1.0

        def _forward(x, W, bias, rw1, rb1, rw2, rb2, A, B, gates):
            lead = x.shape[:-1]
            x_flat = x.reshape(-1, D_IN)
            n = x_flat.shape[0]
            feat = jax.lax.stop_gradient(x_flat)
            h = jax.nn.silu(feat @ rw1.T + rb1)
            logits = (h @ rw2.T + rb2)[:, :N_EXPERTS] + gates[None, :]
            topv, topi = jax.lax.top_k(logits, TOPK)
            sm = jax.nn.softmax(topv, axis=-1)
            rows = jnp.arange(n)[:, None]
            coeff = jnp.zeros_like(logits).at[rows, topi].set(sm)
            base = x_flat @ W.T + bias
            xa = jnp.einsum('ni,eri->ner', x_flat, A)
            wxa = xa * coeff[:, :, None]
            delta = jnp.einsum('ner,eor->no', wxa, B)
            out = base + ALPHA * delta
            return out.reshape(*lead, D_OUT)
        return _forward(x, W, bias, rw1, rb1, rw2, rb2, A, B, gates)
    x = x + _L0_ffn_ref(_L0_cond_ref(x, fside_BxSxS_0, fside_BxSxS_0, L0_cond_w, L0_cond_u, cond_512), L0_ffn_W, L0_ffn_bias, L0_ffn_rw1, L0_ffn_rb1, L0_ffn_rw2, L0_ffn_rb2, L0_ffn_A, L0_ffn_B, L0_ffn_gates)
    return x

_drawn_inputs = setup_inputs


def setup_inputs(seed=0):
    import zlib

    import numpy as np

    out = dict(_drawn_inputs(seed))
    spreads = {'L0_ffn_rb1': (0.0, 0.8), 'L0_ffn_rb2': (0.0, 0.8), 'L0_ffn_gates': (1.0, 0.6)}
    factors = {'L0_ffn_bias': 2.898,
     'L0_ffn_rw1': 8.0,
     'L0_ffn_rw2': 8.0,
     'L0_ffn_A': 3.434,
     'L0_ffn_B': 3.427}
    for name, (base, spread) in spreads.items():
        noise = np.random.default_rng([zlib.crc32(name.encode()), seed]).standard_normal(out[name].shape)
        drawn = base * np.exp(spread * noise) if base else spread * noise
        out[name] = jnp.asarray(drawn.astype(out[name].dtype))
    for name, factor in factors.items():
        out[name] = (out[name] * factor).astype(out[name].dtype)
    return out
```

```python
import numpy as np
import concourse.bass as bass
from concourse import mybir
from contextlib import ExitStack


def bidirectional_decay_mix_with_routed_lora(nc, x_cm, x_tm, f_cm, cond, w, u, weights, bias, rb1, rw2, rb2, gates,
                                             ident, iota, out):
    fp32, fp32r, u32 = mybir.dt.float32, mybir.dt.float32r, mybir.dt.uint32
    ALU = mybir.AluOpType
    ACT = mybir.ActivationFunctionType
    AX = mybir.AxisListType

    P = 128
    UNITS, _, T = f_cm.shape
    TILES, _, D = x_tm.shape
    NB, TD = cond.shape
    CB = UNITS // NB
    LAG = CB
    E = gates.shape[-1]
    HID = rb1.shape[-1]
    ER = 2 * P
    SM = ER + HID
    WC = D + SM
    HALF = D // 2
    CHUNK = weights.shape[1] // CB
    STAGE = 3 * T
    EXP30 = float(np.float32(np.exp(30.0)))
    DEN_MIN_INV = 1e8

    with ExitStack() as ctx:
        def sb(name, shape, dt=fp32):
            return ctx.enter_context(nc.sbuf_tensor(name, shape, dt))

        def pb(name, shape, dt=fp32):
            return ctx.enter_context(nc.psum_tensor(name, shape, dt))

        def sem(name):
            return ctx.enter_context(nc.semaphore(name))

        w_hi = sb("w_hi", [P, weights.shape[1]], fp32r)
        w_lo = sb("w_lo", [P, weights.shape[1]], fp32r)
        y = sb("y", [P, 2 * CB, T])
        y_hi = sb("y_hi", [P, 2, CB, P], fp32r)
        y_lo = sb("y_lo", [P, 2, CB, P], fp32r)
        kv = sb("kv", [P, 2, T])
        den = sb("den", [P, T])
        num = sb("num", [P, T])
        eu = sb("eu", [P, 2, T])
        sig = sb("sig", [P, T])
        xo = sb("xo", [P, 2, HALF])
        bias_sb = sb("bias_sb", [P, D])
        wx = sb("wx", [P, ER])
        wt_hi = sb("wt_hi", [P, 2, P], fp32r)
        wt_lo = sb("wt_lo", [P, 2, P], fp32r)
        ident_sb = sb("ident_sb", [P, P])
        ht = sb("ht", [HID, P])
        hs_wide = sb("hs_wide", [P, P])
        hs = hs_wide[:, 0:HID]
        gate = sb("gate", [P, 2])
        hg = sb("hg", [P, HID])
        rb1_sb = sb("rb1_sb", [P, HID])
        rw2_sb = sb("rw2_sb", [HID, E])
        rb2_sb = sb("rb2_sb", [P, E])
        gates_sb = sb("gates_sb", [P, E])
        rbg = sb("rbg", [P, E])
        iota_sb = sb("iota_sb", [P, E])
        lg = sb("lg", [P, E])
        coef = sb("coef", [P, 3, E])
        top = sb("top", [P, 8])
        topi = sb("topi", [P, 8], u32)
        topf = sb("topf", [P, 2])
        pr = sb("pr", [P, 4])
        w_sb = sb("w_sb", [P, CB])
        u_sb = sb("u_sb", [P, CB])
        u_g = sb("u_g", [P, NB, CB])
        d_g = sb("d_g", [P, NB, CB])
        dd = sb("dd", [P, 2, NB, CB])
        delta_g = sb("delta_g", [P, NB, CB])
        rdelta_g = sb("rdelta_g", [P, NB, CB])
        gain_g = sb("gain_g", [P, NB, CB])
        tf = sb("tf", [P, 4, NB])
        tiny = sb("tiny", [P, 1])

        out_ps = pb("out_ps", [P, 4, HALF])
        small_ps = pb("small_ps", [P, 2, 512])
        rt_ps = pb("rt_ps", [P, 512])
        d_ps = pb("d_ps", [P, 512])

        w_raw = y[:, :, :].rearrange("p s t -> p (s t)")[:, STAGE:STAGE + weights.shape[1]]
        cond_sb = y[:, 1, :]
        flat = lambda t: t[:, :, :].rearrange("p b c -> p (b c)")
        u_f, delta_f, rdelta_f, gain_f = flat(u_g), flat(delta_g), flat(rdelta_g), flat(gain_g)

        params_in = sem("params_in")
        w_in = sem("w_in")
        k_in = [sem("k_in0"), sem("k_in1")]
        r_in = sem("r_in")
        x_in = [sem("x_in0"), sem("x_in1")]
        out_stored = [sem("out_stored0"), sem("out_stored1")]
        setup_act = sem("setup_act")
        setup_dve = sem("setup_dve")
        consts_ready = sem("consts_ready")
        w_hi_ready = sem("w_hi_ready")
        w_lo_ready = sem("w_lo_ready")
        e1_ready = sem("e1_ready")
        e2_ready = sem("e2_ready")
        e1_scaled = sem("e1_scaled")
        p1_ready = sem("p1_ready")
        p2_ready = sem("p2_ready")
        den_fwd = sem("den_fwd")
        num_fwd = sem("num_fwd")
        den_last = sem("den_last")
        num_last = sem("num_last")
        den_bwd = sem("den_bwd")
        num_bwd = sem("num_bwd")
        den_ready = sem("den_ready")
        n_ready = sem("n_ready")
        log_ready = sem("log_ready")
        q_ready = sem("q_ready")
        ratio_ready = sem("ratio_ready")
        sig_ready = sem("sig_ready")
        y_ready = sem("y_ready")
        hi_ready = sem("hi_ready")
        lo_ready = sem("lo_ready")
        split_used = sem("split_used")
        small_done = sem("small_done")
        hs_ready = sem("hs_ready")
        hg_ready = sem("hg_ready")
        h_ready = sem("h_ready")
        ht_done = sem("ht_done")
        ht_ready = sem("ht_ready")
        logits_done = sem("logits_done")
        lg_ready = sem("lg_ready")
        top_ready = sem("top_ready")
        topi_ready = sem("topi_ready")
        ex_ready = sem("ex_ready")
        chain = sem("chain")
        wx_ready = sem("wx_ready")
        wt_done = sem("wt_done")
        wt_hi_ready = sem("wt_hi_ready")
        wt_lo_ready = sem("wt_lo_ready")
        out_done = sem("out_done")
        xb_ready = sem("xb_ready")
        evacuated = sem("evacuated")

        def sl(i):
            return bass.ds(i, 1)

        def row(t, i):
            return t[:, sl(i), :].rearrange("p a t -> p (a t)")

        def rev(a):
            return a[:, T - 2::-1]

        def tile_of_y(t):
            base = (t // CB) % 2 * CB
            return y[:, bass.ds(base, CB), bass.ds(t % CB * P, P)]

        block = ctx.enter_context(nc.Block())

        @block.sync
        def _(sp):
            small = [(w_sb[:], w), (u_sb[:], u),
                     (cond_sb, cond.rearrange("b t -> (b t)").partition_broadcast(P)),
                     (rb1_sb[:], rb1.partition_broadcast(P)), (rb2_sb[:], rb2.partition_broadcast(P)),
                     (gates_sb[:], gates.partition_broadcast(P)), (bias_sb[:], bias.partition_broadcast(P)),
                     (iota_sb[:], iota.partition_broadcast(P)), (ident_sb[:], ident), (rw2_sb[:], rw2)]
            for dst, src in small:
                sp.dma_start(dst, src).then_inc(params_in, 16)
            sp.dma_start(kv[:, 0, :], f_cm[0]).then_inc(k_in[0], 16)
            sp.dma_start(kv[:, 1, :], f_cm[1]).then_inc(k_in[1], 16)
            sp.dma_start(sig[:], x_cm[0]).then_inc(r_in, 16)
            for n in range(CB):
                sp.dma_start(w_raw[:, n * CHUNK:(n + 1) * CHUNK],
                             weights[:, n * CHUNK:(n + 1) * CHUNK]).then_inc(w_in, 16)

            def load_k(g, par):
                sp.wait_ge(n_ready, g - 1)
                sp.dma_start(kv[:, par, :], f_cm[sl(g)].rearrange("a p t -> (a p) t")).then_inc(k_in[par], 16)

            def load_r(g):
                sp.wait_ge(y_ready, g)
                sp.dma_start(sig[:], x_cm[sl(g)].rearrange("a p t -> (a p) t")).then_inc(r_in, 16)

            def store(t):
                for h in range(2):
                    sp.wait_ge(evacuated, 2 * t + h + 1)
                    sp.dma_start(out[sl(t), :, h * HALF:(h + 1) * HALF].rearrange("a p c -> (a p) c"),
                                 xo[:, h, :]).then_inc(out_stored[h], 16)

            def load_x(t, first=False):
                for h in range(2):
                    if not first:
                        sp.wait_ge(out_stored[h], 16 * t)
                    sp.dma_start(xo[:, h, :],
                                 x_tm[sl(t), :, h * HALF:(h + 1) * HALF].rearrange("a p c -> (a p) c")
                                 ).then_inc(x_in[h], 16)

            load_x(0, first=True)

            def step(g, par, k=True, r=True, st=True, lx=True):
                if k:
                    load_k(g + 1, par)
                if st:
                    store(g - LAG - 2)
                if r:
                    load_r(g)
                if lx:
                    load_x(g - LAG - 1)

            with sp.Fori(1, LAG, 2) as g:
                step(g, 0, st=False, lx=False)
                step(g + 1, 1, st=False, lx=False)
            step(LAG + 1, 0, st=False, lx=False)
            step(LAG + 2, 1)
            with sp.Fori(LAG + 3, UNITS - 2, 2) as g:
                step(g, 0)
                step(g + 1, 1)
            step(UNITS - 1, 0, k=False)
            with sp.Fori(UNITS, UNITS + LAG + 1) as g:
                step(g, 0, k=False, r=False)
            store(TILES - 1)
            for h in range(2):
                sp.wait_ge(out_stored[h], 16 * TILES)

        @block.scalar
        def _(act):
            act.wait_ge(params_in, 160)
            nc.scalar.activation(w_sb[:], w_sb[:], ACT.Exp).then_inc(setup_act, 1)
            act.wait_ge(setup_act, 1)
            nc.scalar.activation(w_sb[:], w_sb[:], ACT.Exp, scale=-1.0).then_inc(setup_act, 1)
            act.wait_ge(setup_dve, 1)
            nc.scalar.activation(tf[:, 1, :], tf[:, 0, :], ACT.Sigmoid).then_inc(setup_act, 1)

            def exp_k(g, par, first=False):
                act.wait_ge(k_in[par], 16 * (g // 2 + 1))
                if not first:
                    act.wait_ge(den_ready, g)
                nc.scalar.activation(den[:], kv[:, par, :], ACT.Exp).then_inc(e1_ready, 1)

            def exp_uk(g, par, first=False):
                act.wait_ge(k_in[par], 16 * (g // 2 + 1))
                if not first:
                    act.wait_ge(ratio_ready, g - 1)
                nc.scalar.activation(eu[:, par, :], kv[:, par, :], ACT.Exp,
                                     bias=u_f[:, sl(g)]).then_inc(e2_ready, 1)

            def inverse(g, par):
                act.wait_ge(den_ready, g + 1)
                nc.scalar.activation(eu[:, par, :], eu[:, par, :], ACT.Ln, bias=tiny[:]).then_inc(log_ready, 1)
                act.wait_ge(log_ready, g + 1)
                nc.scalar.activation(eu[:, par, :], eu[:, par, :], ACT.Exp, scale=-1.0).then_inc(q_ready, 1)

            def weights_hi(n):
                nc.scalar.activation(w_hi[:, bass.ds(n * CHUNK, CHUNK)], w_raw[:, bass.ds(n * CHUNK, CHUNK)],
                                     ACT.Copy).then_inc(w_hi_ready, 1)

            def split_hi(t, par, first=False):
                act.wait_ge(y_ready, (t // CB + 1) * CB)
                if not first:
                    act.wait_ge(split_used, t - 1)
                nc.scalar.activation(y_hi[:, par, :, :], tile_of_y(t), ACT.Copy).then_inc(hi_ready, 1)

            def step(g, par, ek=True, inv=True, hi=True, first_hi=False, route=True, ex=True, s=True, hid=True):
                t = g - LAG
                if ek:
                    exp_k(g, par)
                if inv:
                    inverse(g - 1, 1 - par)
                if hi:
                    split_hi(t, par, first_hi)
                if route:
                    act.wait_ge(ht_done, t)
                    nc.scalar.copy(ht[:], rt_ps[0:HID, 0:P]).then_inc(ht_ready, 1)
                if ex:
                    exp_uk(g + 1, 1 - par)
                if route:
                    act.wait_ge(top_ready, t)
                    nc.scalar.activation(pr[:, 0:1], top[:, 0:1], ACT.Exp, bias=top[:, 1:2],
                                         scale=-1.0).then_inc(ex_ready, 1)
                    act.wait_ge(wt_done, t)
                    nc.scalar.copy(wt_hi[:, :, :], rt_ps[:, ER:2 * ER].rearrange("p (a t) -> p a t", a=2)
                                   ).then_inc(wt_hi_ready, 1)
                if s:
                    act.wait_ge(r_in, 16 * (g + 1))
                    nc.scalar.activation(sig[:], sig[:], ACT.Sigmoid).then_inc(sig_ready, 1)
                if hid:
                    act.wait_ge(hs_ready, t + 1)
                    nc.scalar.activation(hg[:], hs, ACT.Sigmoid).then_inc(hg_ready, 1)

            act.wait_ge(consts_ready, 1)
            exp_k(0, 0, first=True)
            exp_uk(0, 0, first=True)
            exp_uk(1, 1, first=True)
            step(0, 0, ek=False, inv=False, hi=False, route=False, ex=False, hid=False)
            act.wait_ge(w_in, 16 * CB)
            weights_hi(0)
            with act.Fori(1, LAG - 2, 2) as g:
                step(g, 1, hi=False, route=False, hid=False)
                weights_hi(g)
                step(g + 1, 0, hi=False, route=False, hid=False)
                weights_hi(g + 1)
            step(LAG - 1, 1, hi=False, route=False, hid=False)
            weights_hi(LAG - 1)
            step(LAG, 0, first_hi=True, route=False)
            step(LAG + 1, 1, first_hi=True)
            with act.Fori(LAG + 2, UNITS - 3, 2) as g:
                step(g, 0)
                step(g + 1, 1)
            step(UNITS - 2, 0)
            step(UNITS - 1, 1, ex=False)
            step(UNITS, 0, ek=False, ex=False, s=False)
            with act.Fori(UNITS + 1, UNITS + LAG - 2, 2) as g:
                step(g, 1, ek=False, inv=False, ex=False, s=False)
                step(g + 1, 0, ek=False, inv=False, ex=False, s=False)
            step(UNITS + LAG - 1, 1, ek=False, inv=False, ex=False, s=False)
            step(UNITS + LAG, 0, ek=False, inv=False, hi=False, ex=False, s=False, hid=False)

        @block.gpsimd
        def _(pool):
            def weights_lo(n):
                pool.wait_ge(w_hi_ready, n + 1)
                c = bass.ds(n * CHUNK, CHUNK)
                nc.gpsimd.tensor_tensor(w_lo[:, c], w_raw[:, c], w_hi[:, c].bitcast(fp32),
                                        ALU.subtract).then_inc(w_lo_ready, 1)

            def step(g, par, lo=True, mix=True, x=True, first=False):
                t = g - LAG
                if lo:
                    pool.wait_ge(hi_ready, t + 1)
                    nc.gpsimd.tensor_tensor(y_lo[:, par, :, :], tile_of_y(t), y_hi[:, par, :, :].bitcast(fp32),
                                            ALU.subtract).then_inc(lo_ready, 1)
                if mix:
                    if not first:
                        pool.wait_ge(n_ready, g)
                    pool.wait_ge(e1_scaled, g + 1)
                    nc.gpsimd.tensor_tensor(num[:], den[:], kv[:, par, :],
                                            ALU.mult).then_inc(p1_ready, 1)
                if x:
                    for h in range(2):
                        pool.wait_ge(x_in[h], 16 * t)
                        nc.gpsimd.tensor_tensor(xo[:, h, :], xo[:, h, :], bias_sb[:, h * HALF:(h + 1) * HALF],
                                                ALU.add).then_inc(xb_ready, 1)
                if mix:
                    pool.wait_ge(num_bwd, g + 1)
                    pool.wait_ge(p2_ready, g + 1)
                    nc.gpsimd.tensor_tensor(row(y, g % (2 * CB)), num[:], kv[:, par, :],
                                            ALU.add).then_inc(n_ready, 1)

            pool.wait_ge(params_in, 160)
            step(0, 0, lo=False, x=False, first=True)
            weights_lo(0)
            with pool.Fori(1, LAG - 2, 2) as g:
                step(g, 1, lo=False, x=False)
                weights_lo(g)
                step(g + 1, 0, lo=False, x=False)
                weights_lo(g + 1)
            step(LAG - 1, 1, lo=False, x=False)
            weights_lo(LAG - 1)
            step(LAG, 0, x=False)
            step(LAG + 1, 1)
            with pool.Fori(LAG + 2, UNITS - 1, 2) as g:
                step(g, 0)
                step(g + 1, 1)
            with pool.Fori(UNITS, UNITS + LAG - 1, 2) as g:
                step(g, 0, mix=False)
                step(g + 1, 1, mix=False)
            step(UNITS + LAG, 0, lo=False, mix=False)

        @block.vector
        def _(dve):
            count = [0]

            def link(ins):
                count[0] += 1
                ins.then_inc(setup_dve, 1)
                dve.wait_ge(setup_dve, count[0])

            dve.wait_ge(params_in, 160)
            link(nc.vector.reduce_sum(tf[:, 0, :], cond_sb.rearrange("p (b t) -> p b t", b=NB), AX.X))
            dve.wait_ge(setup_act, 3)
            link(nc.vector.tensor_scalar(tf[:, 2, :], tf[:, 1, :], 0.5, 0.5, ALU.mult, ALU.add))
            link(nc.vector.tensor_scalar(tf[:, 3, :], tf[:, 1, :], 0.2, 0.8, ALU.mult, ALU.add))
            over_cb = lambda a: a.unsqueeze(2).to_broadcast([P, NB, CB])
            over_nb = lambda a: a.unsqueeze(1).to_broadcast([P, NB, CB])
            link(nc.vector.tensor_tensor(d_g[:, :, :], over_nb(w_sb[:, :]), over_cb(tf[:, 2, :]), ALU.mult))
            link(nc.vector.tensor_copy(gain_g[:, :, :], over_cb(tf[:, 3, :])))
            link(nc.vector.tensor_copy(u_g[:, :, :], over_nb(u_sb[:, :])))
            link(nc.vector.tensor_copy(d_ps[:, 0:UNITS], flat(d_g)))
            link(nc.vector.tensor_scalar(dd[:, 0, :, :], d_g[:, :, :], -1.0, 1.0, ALU.mult, ALU.add))
            link(nc.vector.tensor_scalar(dd[:, 1, :, :], d_g[:, :, :], 1.0, None, ALU.add))
            link(nc.vector.tensor_tensor(delta_g[:, :, :], dd[:, 0, :, :], dd[:, 1, :, :], ALU.mult))
            link(nc.vector.tensor_scalar(delta_g[:, :, :], delta_g[:, :, :], 1e-12, None, ALU.max))
            link(nc.vector.reciprocal(rdelta_g[:, :, :], delta_g[:, :, :]))
            link(nc.vector.tensor_tensor(rbg[:], rb2_sb[:], gates_sb[:], ALU.add))
            link(nc.vector.memset(tiny[:], 1e-19))
            link(nc.vector.memset(hs_wide[:], 0.0))
            nc.vector.memset(coef[:, 2, 0:1], 0.0).then_inc(consts_ready, 1)

            def decay(g, n):
                return d_ps[:, sl(g)].to_broadcast([P, n])

            def inverse_scale_last(a, g, done):
                last = a[:, T - 1:T]
                nc.vector.tensor_scalar(last, last, rdelta_f[:, sl(g)], None, ALU.mult).then_inc(done, 1)

            def tail(g, par):
                slot = row(y, g % (2 * CB))
                dve.wait_ge(q_ready, g + 1)
                dve.wait_ge(n_ready, g + 1)
                nc.vector.scalar_tensor_tensor(out=slot, in0=eu[:, par, :], scalar=DEN_MIN_INV, in1=slot,
                                               op0=ALU.min, op1=ALU.mult).then_inc(ratio_ready, 1)
                dve.wait_ge(ratio_ready, g + 1)
                dve.wait_ge(sig_ready, g + 1)
                nc.vector.scalar_tensor_tensor(out=slot, in0=slot, scalar=gain_f[:, sl(g)], in1=sig[:],
                                               op0=ALU.mult, op1=ALU.mult).then_inc(y_ready, 1)

            def evacuate(t, tp):
                for h in range(2):
                    if h == 0:
                        dve.wait_ge(out_done, t + 1)
                    dve.wait_ge(xb_ready, 2 * t + h + 1)
                    nc.vector.tensor_tensor(xo[:, h, :], out_ps[:, 2 * tp + h, :], xo[:, h, :],
                                            ALU.add).then_inc(evacuated, 1)

            def route_top(t):
                dve.wait_ge(logits_done, t + 1)
                nc.vector.tensor_tensor(lg[:], rt_ps[:, P:P + E], rbg[:], ALU.add).then_inc(lg_ready, 1)
                dve.wait_ge(lg_ready, t + 1)
                nc.vector.memset(gate[:, 0:1], 0.0)
                nc.vector.max(top[:], lg[:]).then_inc(top_ready, 1)
                dve.wait_ge(top_ready, t + 1)
                nc.vector.memset(gate[:, 1:2], 0.0)
                nc.vector.max_index(topi[:], top[:], lg[:]).then_inc(topi_ready, 1)
                dve.wait_ge(topi_ready, t + 1)
                nc.vector.tensor_copy(topf[:], topi[:, 0:2]).then_inc(chain, 1)

            def route_weights(t, tp):
                CH = 7
                dve.wait_ge(ex_ready, t + 1)
                nc.vector.tensor_scalar(pr[:, 1:2], pr[:, 0:1], 1.0, None, ALU.add).then_inc(chain, 1)
                dve.wait_ge(chain, CH * t + 2)
                nc.vector.reciprocal(pr[:, 2:3], pr[:, 1:2]).then_inc(chain, 1)
                dve.wait_ge(chain, CH * t + 3)
                nc.vector.tensor_tensor(pr[:, 3:4], pr[:, 0:1], pr[:, 2:3], ALU.mult).then_inc(chain, 1)
                nc.vector.tensor_scalar(coef[:, 0, :], iota_sb[:], topf[:, 0:1], pr[:, 2:3],
                                        ALU.is_equal, ALU.mult).then_inc(chain, 1)
                dve.wait_ge(chain, CH * t + 5)
                nc.vector.tensor_scalar(coef[:, 1, :], iota_sb[:], topf[:, 1:2], pr[:, 3:4],
                                        ALU.is_equal, ALU.mult).then_inc(chain, 1)
                dve.wait_ge(chain, CH * t + 6)
                nc.vector.tensor_tensor(coef[:, 2, :], coef[:, 0, :], coef[:, 1, :], ALU.add).then_inc(chain, 1)
                dve.wait_ge(chain, CH * t + 7)
                nc.vector.tensor_tensor(wx[:].rearrange("p (e r) -> p e r", e=E),
                                        small_ps[:, tp, 0:ER].rearrange("p (e r) -> p e r", e=E),
                                        coef[:, 2, :].unsqueeze(2).to_broadcast([P, E, ER // E]),
                                        ALU.mult).then_inc(wx_ready, 1)

            def step(g, par, head=True, fin=True, ev=True, route=True, hid=True):
                t = g - LAG
                if route:
                    dve.wait_ge(hg_ready, t)
                    nc.vector.tensor_tensor(hs, hs, hg[:], ALU.mult).then_inc(h_ready, 1)
                if ev:
                    evacuate(t - 2, par)
                if head:
                    dve.wait_ge(e1_ready, g + 1)
                    nc.vector.tensor_scalar(den[:], den[:], EXP30, delta_f[:, sl(g)],
                                            ALU.min, ALU.mult).then_inc(e1_scaled, 1)
                if fin:
                    tail(g - 1, 1 - par)
                if head:
                    dve.wait_ge(p1_ready, g + 1)
                    nc.vector.tensor_tensor_scan(den[:], decay(g, T), den[:], 0.0,
                                                 ALU.mult, ALU.add).then_inc(den_fwd, 1)
                    dve.wait_ge(e2_ready, g + 1)
                    nc.vector.scalar_tensor_tensor(out=kv[:, par, :], in0=eu[:, par, :], scalar=EXP30,
                                                   in1=kv[:, par, :], op0=ALU.min,
                                                   op1=ALU.mult).then_inc(p2_ready, 1)
                if route:
                    route_top(t - 1)
                if head:
                    nc.vector.tensor_tensor_scan(num[:], decay(g, T), num[:], 0.0,
                                                 ALU.mult, ALU.add).then_inc(num_fwd, 1)
                if route:
                    route_weights(t - 1, 1 - par)
                if head:
                    dve.wait_ge(den_fwd, g + 1)
                    inverse_scale_last(den, g, den_last)
                    dve.wait_ge(num_fwd, g + 1)
                    inverse_scale_last(num, g, num_last)
                    dve.wait_ge(den_last, g + 1)
                    nc.vector.tensor_tensor_scan(rev(den), decay(g, T - 1), rev(den),
                                                 den[:, T - 1:T], ALU.mult, ALU.add).then_inc(den_bwd, 1)
                if hid:
                    dve.wait_ge(small_done, t + 1)
                    nc.vector.tensor_tensor(hs, small_ps[:, par, ER:SM], rb1_sb[:],
                                            ALU.add).then_inc(hs_ready, 1)
                if head:
                    dve.wait_ge(num_last, g + 1)
                    nc.vector.tensor_tensor_scan(rev(num), decay(g, T - 1), rev(num),
                                                 num[:, T - 1:T], ALU.mult, ALU.add).then_inc(num_bwd, 1)
                    dve.wait_ge(den_bwd, g + 1)
                    nc.vector.scalar_tensor_tensor(out=eu[:, par, :], in0=eu[:, par, :], scalar=EXP30,
                                                   in1=den[:], op0=ALU.min,
                                                   op1=ALU.add).then_inc(den_ready, 1)
                if route:
                    dve.wait_ge(wt_hi_ready, t)
                    nc.vector.tensor_tensor(wt_lo[:, :, :], rt_ps[:, ER:2 * ER].rearrange("p (a t) -> p a t", a=2),
                                            wt_hi[:, :, :].bitcast(fp32), ALU.subtract).then_inc(wt_lo_ready, 1)

            step(0, 0, fin=False, ev=False, route=False, hid=False)
            with dve.Fori(1, LAG - 2, 2) as g:
                step(g, 1, ev=False, route=False, hid=False)
                step(g + 1, 0, ev=False, route=False, hid=False)
            step(LAG - 1, 1, ev=False, route=False, hid=False)
            step(LAG, 0, ev=False, route=False)
            step(LAG + 1, 1, ev=False)
            with dve.Fori(LAG + 2, UNITS - 1, 2) as g:
                step(g, 0)
                step(g + 1, 1)
            step(UNITS, 0, head=False)
            with dve.Fori(UNITS + 1, UNITS + LAG - 2, 2) as g:
                step(g, 1, head=False, fin=False)
                step(g + 1, 0, head=False, fin=False)
            step(UNITS + LAG - 1, 1, head=False, fin=False)
            step(UNITS + LAG, 0, head=False, fin=False, hid=False)
            evacuate(TILES - 1, 1)

        @block.tensor
        def _(pe):
            def three(out_ap, lh, ll, rh, rl, start, stop):
                nc.tensor.matmul(out_ap, lh, rh, start=start, stop=False)
                nc.tensor.matmul(out_ap, lh, rl, start=False, stop=False)
                return nc.tensor.matmul(out_ap, ll, rh, start=False, stop=stop)

            def small(t, par, free=True):
                pe.wait_ge(lo_ready, t + 1)
                if free:
                    pe.wait_ge(wx_ready, t - 1)
                for kc in range(CB):
                    c = slice(kc * WC + D, (kc + 1) * WC)
                    last = three(small_ps[:, par, 0:SM], y_hi[:, par, kc, :], y_lo[:, par, kc, :],
                                 w_hi[:, c], w_lo[:, c], kc == 0, kc == CB - 1)
                last.then_inc(small_done, 1)

            def main(t, par, kc):
                for h in range(2):
                    c = slice(kc * WC + h * HALF, kc * WC + (h + 1) * HALF)
                    last = three(out_ps[:, 2 * par + h, :], y_hi[:, par, kc, :], y_lo[:, par, kc, :],
                                 w_hi[:, c], w_lo[:, c], kc == 0, False)
                if kc == CB - 1:
                    last.then_inc(split_used, 1)

            def hidden_transpose(t):
                pe.wait_ge(h_ready, t + 1)
                nc.tensor.transpose(rt_ps[:, 0:P], hs_wide[:], ident_sb[:]).then_inc(ht_done, 1)

            def logits(t):
                pe.wait_ge(ht_ready, t + 1)
                nc.tensor.matmul(rt_ps[:, P:P + E], ht[:], rw2_sb[:], start=True, stop=True).then_inc(logits_done, 1)

            def weighted_transpose(t):
                pe.wait_ge(wx_ready, t + 1)
                for a in range(2):
                    last = nc.tensor.transpose(rt_ps[:, ER + a * P:ER + (a + 1) * P], wx[:, a * P:(a + 1) * P],
                                               ident_sb[:])
                last.then_inc(wt_done, 1)

            def expert(t, par):
                pe.wait_ge(wt_lo_ready, t + 1)
                for h in range(2):
                    for a in range(2):
                        c0 = CB * WC + a * D + h * HALF
                        last = three(out_ps[:, 2 * par + h, :], wt_hi[:, a, :], wt_lo[:, a, :],
                                     w_hi[:, c0:c0 + HALF], w_lo[:, c0:c0 + HALF], False, a == 1)
                last.then_inc(out_done, 1)

            def step(t, par, route=True, free=True):
                small(t, par, free)
                if free:
                    pe.wait_ge(evacuated, 2 * (t - 1))
                if route:
                    hidden_transpose(t - 1)
                main(t, par, 0)
                main(t, par, 1)
                if route:
                    logits(t - 1)
                main(t, par, 2)
                main(t, par, 3)
                if route:
                    weighted_transpose(t - 1)
                main(t, par, 4)
                main(t, par, 5)
                if route:
                    expert(t - 1, 1 - par)
                main(t, par, 6)
                main(t, par, 7)

            pe.wait_ge(w_lo_ready, CB)
            step(0, 0, route=False, free=False)
            step(1, 1, free=False)
            with pe.Fori(2, TILES - 1, 2) as t:
                step(t, 0)
                step(t + 1, 1)
            hidden_transpose(TILES - 1)
            logits(TILES - 1)
            weighted_transpose(TILES - 1)
            expert(TILES - 1, 1)


def kernel(x, fside_BxSxS_0, cond_512, L0_cond_w, L0_cond_u, L0_ffn_W, L0_ffn_bias, L0_ffn_rw1, L0_ffn_rb1,
           L0_ffn_rw2, L0_ffn_rb2, L0_ffn_A, L0_ffn_B, L0_ffn_gates):
    import concourse.bacc as bacc
    from concourse.bass_utils import run_bass_kernel_spmd

    P = 128
    x = np.asarray(x)
    f = np.asarray(fside_BxSxS_0)
    nb, t, c = x.shape
    cb = c // P
    e, r, _ = L0_ffn_A.shape
    er = e * r
    hid = L0_ffn_rw1.shape[0]
    first = np.concatenate([np.asarray(L0_ffn_W).T, np.asarray(L0_ffn_A).reshape(er, c).T,
                            np.asarray(L0_ffn_rw1).T], axis=1)
    first = first.reshape(cb, P, -1).transpose(1, 0, 2).reshape(P, -1)
    second = np.asarray(L0_ffn_B).transpose(0, 2, 1).reshape(er // P, P, c).transpose(1, 0, 2).reshape(P, -1)
    arrays = {
        "x_cm": x.transpose(0, 2, 1).reshape(nb * cb, P, t),
        "x_tm": x.reshape(nb * t // P, P, c),
        "f_cm": f.transpose(0, 2, 1).reshape(nb * cb, P, t),
        "cond": np.asarray(cond_512),
        "w": np.asarray(L0_cond_w).reshape(cb, P).T,
        "u": np.asarray(L0_cond_u).reshape(cb, P).T,
        "weights": np.concatenate([first, second], axis=1),
        "bias": np.asarray(L0_ffn_bias),
        "rb1": np.asarray(L0_ffn_rb1),
        "rw2": np.asarray(L0_ffn_rw2)[:e].T,
        "rb2": np.asarray(L0_ffn_rb2)[:e],
        "gates": np.asarray(L0_ffn_gates),
        "ident": np.eye(P, dtype=np.float32),
        "iota": np.arange(e, dtype=np.float32),
    }
    arrays = {name: np.ascontiguousarray(a) for name, a in arrays.items()}
    nc = bacc.Bacc("TRN2", target_bir_lowering=False, num_devices=1, dynamic_dma_scratch_size=1024)
    args = [nc.dram_tensor(name, a.shape, mybir.dt.from_np(a.dtype), kind="ExternalInput").ap()
            for name, a in arrays.items()]
    out = nc.dram_tensor("out", (nb * t // P, P, c), mybir.dt.float32, kind="ExternalOutput").ap()
    bidirectional_decay_mix_with_routed_lora(nc, *args, out)
    result = run_bass_kernel_spmd(nc, [arrays], core_ids=[0])
    return result.results[0]["out"].reshape(nb, t, c)
```

```python
import numpy as np
import concourse.bass as bass
from concourse import mybir
from contextlib import ExitStack


def bidirectional_decay_mix_with_routed_lora(nc, x_cm, x_tm, f_cm, cond, w, u, weights, bias, rb1, rw2, rb2, gates,
                                             ident, iota, out):
    fp32, fp32r, u32 = mybir.dt.float32, mybir.dt.float32r, mybir.dt.uint32
    ALU = mybir.AluOpType
    ACT = mybir.ActivationFunctionType
    AX = mybir.AxisListType

    P = 128
    UNITS, _, T = f_cm.shape
    TILES, _, D = x_tm.shape
    NB, TD = cond.shape
    CB = UNITS // NB
    LAG = CB + 1
    E = gates.shape[-1]
    HID = rb1.shape[-1]
    ER = 2 * P
    SM = ER + HID
    WC = D + SM
    HALF = D // 2
    CHUNKS = 5
    CHUNK = weights.shape[1] // CHUNKS
    STAGE = 3 * T
    EXP30 = float(np.float32(np.exp(30.0)))
    DEN_MIN_INV = 1e8

    with ExitStack() as ctx:
        def sb(name, shape, dt=fp32):
            return ctx.enter_context(nc.sbuf_tensor(name, shape, dt))

        def pb(name, shape, dt=fp32):
            return ctx.enter_context(nc.psum_tensor(name, shape, dt))

        def sem(name):
            return ctx.enter_context(nc.semaphore(name))

        w_hi = sb("w_hi", [P, weights.shape[1]], fp32r)
        w_lo = sb("w_lo", [P, weights.shape[1]], fp32r)
        y = sb("y", [P, 2 * CB, T])
        y_hi = sb("y_hi", [P, 2, CB, P], fp32r)
        y_lo = sb("y_lo", [P, 2, CB, P], fp32r)
        kv = sb("kv", [P, 2, T])
        den = sb("den", [P, T])
        num = sb("num", [P, T])
        eu = sb("eu", [P, 2, T])
        sig = sb("sig", [P, T])
        xo = sb("xo", [P, 2, HALF])
        bias_sb = sb("bias_sb", [P, D])
        wx = sb("wx", [P, ER])
        wt_hi = sb("wt_hi", [P, 2, P], fp32r)
        wt_lo = sb("wt_lo", [P, 2, P], fp32r)
        ident_sb = sb("ident_sb", [P, P])
        ht = sb("ht", [HID, P])
        hs_wide = sb("hs_wide", [P, P])
        hs = hs_wide[:, 0:HID]
        gate = sb("gate", [P, 2])
        hg = sb("hg", [P, HID])
        rb1_sb = sb("rb1_sb", [P, HID])
        rw2_sb = sb("rw2_sb", [HID, E])
        rb2_sb = sb("rb2_sb", [P, E])
        gates_sb = sb("gates_sb", [P, E])
        rbg = sb("rbg", [P, E])
        iota_sb = sb("iota_sb", [P, E])
        lg = sb("lg", [P, E])
        coef = sb("coef", [P, 3, E])
        top = sb("top", [P, 8])
        topi = sb("topi", [P, 8], u32)
        topf = sb("topf", [P, 2])
        pr = sb("pr", [P, 4])
        w_sb = sb("w_sb", [P, CB])
        u_sb = sb("u_sb", [P, CB])
        u_g = sb("u_g", [P, NB, CB])
        d_g = sb("d_g", [P, NB, CB])
        dd = sb("dd", [P, 2, NB, CB])
        delta_g = sb("delta_g", [P, NB, CB])
        rdelta_g = sb("rdelta_g", [P, NB, CB])
        gain_g = sb("gain_g", [P, NB, CB])
        tf = sb("tf", [P, 4, NB])
        tiny = sb("tiny", [P, 1])

        out_ps = pb("out_ps", [P, 4, HALF])
        small_ps = pb("small_ps", [P, 2, 512])
        rt_ps = pb("rt_ps", [P, 512])
        d_ps = pb("d_ps", [P, 512])

        w_raw = y[:, :, :].rearrange("p s t -> p (s t)")[:, STAGE:STAGE + weights.shape[1]]
        cond_sb = y[:, 1, :]
        flat = lambda t: t[:, :, :].rearrange("p b c -> p (b c)")
        u_f, delta_f, rdelta_f, gain_f = flat(u_g), flat(delta_g), flat(rdelta_g), flat(gain_g)

        late = [(rb1_sb[:], rb1.partition_broadcast(P)), (rb2_sb[:], rb2.partition_broadcast(P)),
                (gates_sb[:], gates.partition_broadcast(P)), (bias_sb[:], bias.partition_broadcast(P)),
                (iota_sb[:], iota.partition_broadcast(P)), (ident_sb[:], ident), (rw2_sb[:], rw2)]
        LATE = len(late)

        params_in = sem("params_in")
        late_in = sem("late_in")
        w_in = sem("w_in")
        k_in = [sem("k_in0"), sem("k_in1")]
        r_in = sem("r_in")
        x_in = [sem("x_in0"), sem("x_in1")]
        out_stored = [sem("out_stored0"), sem("out_stored1")]
        setup_act = sem("setup_act")
        setup_dve = sem("setup_dve")
        rbg_ready = sem("rbg_ready")
        consts_ready = sem("consts_ready")
        w_hi_ready = sem("w_hi_ready")
        w_lo_ready = sem("w_lo_ready")
        e1_ready = sem("e1_ready")
        e2_ready = sem("e2_ready")
        e1_scaled = sem("e1_scaled")
        p1_ready = sem("p1_ready")
        p2_ready = sem("p2_ready")
        den_fwd = sem("den_fwd")
        num_fwd = sem("num_fwd")
        den_last = sem("den_last")
        num_last = sem("num_last")
        den_bwd = sem("den_bwd")
        num_bwd = sem("num_bwd")
        den_ready = sem("den_ready")
        n_ready = sem("n_ready")
        log_ready = sem("log_ready")
        q_ready = sem("q_ready")
        ratio_ready = sem("ratio_ready")
        sig_ready = sem("sig_ready")
        y_ready = sem("y_ready")
        hi_ready = sem("hi_ready")
        lo_ready = sem("lo_ready")
        split_used = sem("split_used")
        small_done = sem("small_done")
        hs_ready = sem("hs_ready")
        hg_ready = sem("hg_ready")
        h_ready = sem("h_ready")
        ht_done = sem("ht_done")
        ht_ready = sem("ht_ready")
        logits_done = sem("logits_done")
        lg_ready = sem("lg_ready")
        top_ready = sem("top_ready")
        topi_ready = sem("topi_ready")
        ex_ready = sem("ex_ready")
        chain = sem("chain")
        wx_ready = sem("wx_ready")
        wt_done = sem("wt_done")
        wt_hi_ready = sem("wt_hi_ready")
        wt_lo_ready = sem("wt_lo_ready")
        out_done = sem("out_done")
        xb_ready = sem("xb_ready")
        evacuated = sem("evacuated")

        def sl(i):
            return bass.ds(i, 1)

        def row(t, i):
            return t[:, sl(i), :].rearrange("p a t -> p (a t)")

        def rev(a):
            return a[:, T - 2::-1]

        def tile_of_y(t):
            base = (t // CB) % 2 * CB
            return y[:, bass.ds(base, CB), bass.ds(t % CB * P, P)]

        block = ctx.enter_context(nc.Block())

        @block.sync
        def _(sp):
            sp.dma_start(cond_sb, cond.rearrange("b t -> (b t)").partition_broadcast(P)).then_inc(params_in, 16)
            sp.dma_start(kv[:, 0, :], f_cm[0]).then_inc(k_in[0], 16)
            sp.dma_start(w_sb[:], w).then_inc(params_in, 16)
            sp.dma_start(u_sb[:], u).then_inc(params_in, 16)
            sp.dma_start(kv[:, 1, :], f_cm[1]).then_inc(k_in[1], 16)
            sp.dma_start(sig[:], x_cm[0]).then_inc(r_in, 16)
            for dst, src in late:
                sp.dma_start(dst, src).then_inc(late_in, 16)
            for n in range(CHUNKS):
                sp.dma_start(w_raw[:, n * CHUNK:(n + 1) * CHUNK],
                             weights[:, n * CHUNK:(n + 1) * CHUNK]).then_inc(w_in, 16)

            def load_k(g, par):
                sp.wait_ge(n_ready, g - 1)
                sp.dma_start(kv[:, par, :], f_cm[sl(g)].rearrange("a p t -> (a p) t")).then_inc(k_in[par], 16)

            def load_r(g):
                sp.wait_ge(y_ready, g)
                sp.dma_start(sig[:], x_cm[sl(g)].rearrange("a p t -> (a p) t")).then_inc(r_in, 16)

            def store(t):
                for h in range(2):
                    sp.wait_ge(evacuated, 2 * t + h + 1)
                    sp.dma_start(out[sl(t), :, h * HALF:(h + 1) * HALF].rearrange("a p c -> (a p) c"),
                                 xo[:, h, :]).then_inc(out_stored[h], 16)

            def load_x(t, first=False):
                for h in range(2):
                    if not first:
                        sp.wait_ge(out_stored[h], 16 * t)
                    sp.dma_start(xo[:, h, :],
                                 x_tm[sl(t), :, h * HALF:(h + 1) * HALF].rearrange("a p c -> (a p) c")
                                 ).then_inc(x_in[h], 16)

            def step(g, par, k=True, r=True, st=True, lx=True, first=False):
                t = g - LAG
                if k:
                    load_k(g + 1, 1 - par)
                if st:
                    store(t - 2)
                if r:
                    load_r(g)
                if lx:
                    load_x(t - 1, first)

            with sp.Fori(1, LAG - 1, 2) as g:
                step(g, 1, st=False, lx=False)
                step(g + 1, 0, st=False, lx=False)
            step(LAG, 1, st=False, lx=False)
            step(LAG + 1, 0, st=False, first=True)
            with sp.Fori(LAG + 2, UNITS - 2, 2) as g:
                step(g, 1)
                step(g + 1, 0)
            step(UNITS - 1, 1, k=False)
            with sp.Fori(UNITS, UNITS + LAG + 1) as g:
                step(g, 0, k=False, r=False)
            store(TILES - 1)
            for h in range(2):
                sp.wait_ge(out_stored[h], 16 * TILES)

        @block.scalar
        def _(act):
            def exp_k(g, par, first=False):
                act.wait_ge(k_in[par], 16 * (g // 2 + 1))
                if not first:
                    act.wait_ge(den_ready, g)
                nc.scalar.activation(den[:], kv[:, par, :], ACT.Exp).then_inc(e1_ready, 1)

            nc.scalar.preload_act_table_set("natural_log_exp_and_others")
            exp_k(0, 0, first=True)
            act.wait_ge(params_in, 48)
            nc.scalar.activation(w_sb[:], w_sb[:], ACT.Exp).then_inc(setup_act, 1)
            act.wait_ge(setup_act, 1)
            nc.scalar.activation(w_sb[:], w_sb[:], ACT.Exp, scale=-1.0).then_inc(setup_act, 1)
            act.wait_ge(setup_dve, 1)
            nc.scalar.activation(tf[:, 1, :], tf[:, 0, :], ACT.Sigmoid).then_inc(setup_act, 1)

            def exp_uk(g, par, first=False):
                act.wait_ge(k_in[par], 16 * (g // 2 + 1))
                if not first:
                    act.wait_ge(ratio_ready, g - 1)
                nc.scalar.activation(eu[:, par, :], kv[:, par, :], ACT.Exp,
                                     bias=u_f[:, sl(g)]).then_inc(e2_ready, 1)

            def inverse(g, par):
                act.wait_ge(den_ready, g + 1)
                nc.scalar.activation(eu[:, par, :], eu[:, par, :], ACT.Ln, bias=tiny[:]).then_inc(log_ready, 1)
                act.wait_ge(log_ready, g + 1)
                nc.scalar.activation(eu[:, par, :], eu[:, par, :], ACT.Exp, scale=-1.0).then_inc(q_ready, 1)

            def weights_hi(n):
                nc.scalar.activation(w_hi[:, bass.ds(n * CHUNK, CHUNK)], w_raw[:, bass.ds(n * CHUNK, CHUNK)],
                                     ACT.Copy).then_inc(w_hi_ready, 1)

            def split_hi(t, par, first=False):
                act.wait_ge(y_ready, (t // CB + 1) * CB)
                if not first:
                    act.wait_ge(split_used, t - 1)
                nc.scalar.activation(y_hi[:, par, :, :], tile_of_y(t), ACT.Copy).then_inc(hi_ready, 1)

            def sigmoid_r(g):
                act.wait_ge(r_in, 16 * (g + 1))
                nc.scalar.activation(sig[:], sig[:], ACT.Sigmoid).then_inc(sig_ready, 1)

            def step(g, par, ek=True, inv=True, ex=True, hi=True, first_hi=False, route=True, s=True, s_prev=False,
                     hid=True):
                t = g - LAG
                if ek:
                    exp_k(g, par)
                if inv:
                    inverse(g - 1, 1 - par)
                if s_prev:
                    sigmoid_r(g - 1)
                    nc.scalar.preload_act_table_set("natural_log_exp_and_others")
                if ex:
                    exp_uk(g + 1, 1 - par)
                if hi:
                    split_hi(t + 1, par, first_hi)
                if route:
                    act.wait_ge(top_ready, t)
                    nc.scalar.activation(pr[:, 0:1], top[:, 0:1], ACT.Exp, bias=top[:, 1:2],
                                         scale=-1.0).then_inc(ex_ready, 1)
                if s:
                    sigmoid_r(g)
                if hid:
                    act.wait_ge(hs_ready, t + 1)
                    nc.scalar.activation(hg[:], hs, ACT.Sigmoid).then_inc(hg_ready, 1)
                if s or hid:
                    nc.scalar.preload_act_table_set("natural_log_exp_and_others")
                if route:
                    act.wait_ge(wt_done, t)
                    nc.scalar.copy(wt_hi[:, :, :], rt_ps[:, ER:2 * ER].rearrange("p (a t) -> p a t", a=2)
                                   ).then_inc(wt_hi_ready, 1)
                if hid:
                    act.wait_ge(ht_done, t + 1)
                    nc.scalar.copy(ht[:], rt_ps[0:HID, 0:P]).then_inc(ht_ready, 1)

            nc.scalar.preload_act_table_set("natural_log_exp_and_others")
            act.wait_ge(consts_ready, 1)
            exp_uk(0, 0, first=True)
            exp_uk(1, 1, first=True)
            step(1, 1, hi=False, route=False, s=False, s_prev=True, hid=False)
            act.wait_ge(w_in, 16 * CHUNKS)
            weights_hi(0)
            with act.Fori(2, 2 + CHUNKS - 2, 2) as g:
                step(g, 0, hi=False, route=False, s=False, s_prev=True, hid=False)
                weights_hi(g - 1)
                step(g + 1, 1, hi=False, route=False, s=False, s_prev=True, hid=False)
                weights_hi(g)
            step(CB - 2, 0, hi=False, route=False, s=False, s_prev=True, hid=False)
            step(CB - 1, 1, hi=False, route=False, s=False, s_prev=True, hid=False)
            step(LAG - 1, 0, first_hi=True, route=False, s_prev=True, hid=False)
            step(LAG, 1, first_hi=True, route=False)
            with act.Fori(LAG + 1, UNITS - 3, 2) as g:
                step(g, 0)
                step(g + 1, 1)
            step(UNITS - 2, 0)
            step(UNITS - 1, 1, ex=False)
            step(UNITS, 0, ek=False, ex=False, s=False)
            with act.Fori(UNITS + 1, UNITS + CB - 2, 2) as g:
                step(g, 1, ek=False, inv=False, ex=False, s=False)
                step(g + 1, 0, ek=False, inv=False, ex=False, s=False)
            step(UNITS + CB - 1, 1, ek=False, inv=False, ex=False, s=False)
            step(UNITS + CB, 0, ek=False, inv=False, ex=False, hi=False, s=False)
            step(UNITS + LAG, 1, ek=False, inv=False, ex=False, hi=False, s=False, hid=False)

        @block.gpsimd
        def _(pool):
            def weights_lo(n):
                pool.wait_ge(w_hi_ready, n + 1)
                c = bass.ds(n * CHUNK, CHUNK)
                nc.gpsimd.tensor_tensor(w_lo[:, c], w_raw[:, c], w_hi[:, c].bitcast(fp32),
                                        ALU.subtract).then_inc(w_lo_ready, 1)

            def step(g, par, lo=True, mix=True, x=True, p1=True):
                t = g - LAG
                if mix and p1:
                    pool.wait_ge(n_ready, g)
                    pool.wait_ge(e1_scaled, g + 1)
                    nc.gpsimd.tensor_tensor(num[:], den[:], kv[:, par, :], ALU.mult).then_inc(p1_ready, 1)
                if lo:
                    pool.wait_ge(hi_ready, t + 2)
                    nc.gpsimd.tensor_tensor(y_lo[:, par, :, :], tile_of_y(t + 1), y_hi[:, par, :, :].bitcast(fp32),
                                            ALU.subtract).then_inc(lo_ready, 1)
                if x:
                    for h in range(2):
                        pool.wait_ge(x_in[h], 16 * t)
                        nc.gpsimd.tensor_tensor(xo[:, h, :], xo[:, h, :], bias_sb[:, h * HALF:(h + 1) * HALF],
                                                ALU.add).then_inc(xb_ready, 1)
                if mix:
                    pool.wait_ge(num_bwd, g + 1)
                    pool.wait_ge(p2_ready, g + 1)
                    nc.gpsimd.tensor_tensor(row(y, g % (2 * CB)), num[:], kv[:, par, :],
                                            ALU.add).then_inc(n_ready, 1)

            step(0, 0, lo=False, x=False, p1=False)
            step(1, 1, lo=False, x=False, p1=False)
            with pool.Fori(2, 2 + CHUNKS - 2, 2) as g:
                weights_lo(g - 2)
                step(g, 0, lo=False, x=False, p1=False)
                weights_lo(g - 1)
                step(g + 1, 1, lo=False, x=False, p1=False)
            weights_lo(CHUNKS - 1)
            step(1 + CHUNKS, 0, lo=False, x=False, p1=False)
            step(2 + CHUNKS, 1, lo=False, x=False, p1=False)
            pool.wait_ge(late_in, 16 * LATE)
            step(LAG - 1, 0, x=False)
            step(LAG, 1, x=False)
            with pool.Fori(LAG + 1, UNITS - 1, 2) as g:
                step(g, 0)
                step(g + 1, 1)
            with pool.Fori(UNITS, UNITS + CB - 1, 2) as g:
                step(g, 0, mix=False)
                step(g + 1, 1, mix=False)
            step(UNITS + CB, 0, lo=False, mix=False)
            step(UNITS + LAG, 1, lo=False, mix=False)

        @block.vector
        def _(dve):
            count = [0]

            def link(ins):
                count[0] += 1
                ins.then_inc(setup_dve, 1)
                dve.wait_ge(setup_dve, count[0])

            dve.wait_ge(params_in, 48)
            link(nc.vector.reduce_sum(tf[:, 0, :], cond_sb.rearrange("p (b t) -> p b t", b=NB), AX.X))
            dve.wait_ge(setup_act, 3)
            link(nc.vector.tensor_scalar(tf[:, 2, :], tf[:, 1, :], 0.5, 0.5, ALU.mult, ALU.add))
            link(nc.vector.tensor_scalar(tf[:, 3, :], tf[:, 1, :], 0.2, 0.8, ALU.mult, ALU.add))
            over_cb = lambda a: a.unsqueeze(2).to_broadcast([P, NB, CB])
            over_nb = lambda a: a.unsqueeze(1).to_broadcast([P, NB, CB])
            link(nc.vector.tensor_tensor(d_g[:, :, :], over_nb(w_sb[:, :]), over_cb(tf[:, 2, :]), ALU.mult))
            link(nc.vector.tensor_copy(gain_g[:, :, :], over_cb(tf[:, 3, :])))
            link(nc.vector.tensor_copy(u_g[:, :, :], over_nb(u_sb[:, :])))
            link(nc.vector.tensor_copy(d_ps[:, 0:UNITS], flat(d_g)))
            link(nc.vector.tensor_scalar(dd[:, 0, :, :], d_g[:, :, :], -1.0, 1.0, ALU.mult, ALU.add))
            link(nc.vector.tensor_scalar(dd[:, 1, :, :], d_g[:, :, :], 1.0, None, ALU.add))
            link(nc.vector.tensor_tensor(delta_g[:, :, :], dd[:, 0, :, :], dd[:, 1, :, :], ALU.mult))
            link(nc.vector.tensor_scalar(delta_g[:, :, :], delta_g[:, :, :], 1e-12, None, ALU.max))
            link(nc.vector.reciprocal(rdelta_g[:, :, :], delta_g[:, :, :]))
            link(nc.vector.memset(tiny[:], 1e-19))
            link(nc.vector.memset(hs_wide[:], 0.0))
            nc.vector.memset(coef[:, 2, 0:1], 0.0).then_inc(consts_ready, 1)

            def decay(g, n):
                return d_ps[:, sl(g)].to_broadcast([P, n])

            def inverse_scale_last(a, g, done):
                last = a[:, T - 1:T]
                nc.vector.tensor_scalar(last, last, rdelta_f[:, sl(g)], None, ALU.mult).then_inc(done, 1)

            def tail(g, par):
                slot = row(y, g % (2 * CB))
                dve.wait_ge(q_ready, g + 1)
                dve.wait_ge(n_ready, g + 1)
                nc.vector.scalar_tensor_tensor(out=slot, in0=eu[:, par, :], scalar=DEN_MIN_INV, in1=slot,
                                               op0=ALU.min, op1=ALU.mult).then_inc(ratio_ready, 1)
                dve.wait_ge(ratio_ready, g + 1)
                dve.wait_ge(sig_ready, g + 1)
                nc.vector.scalar_tensor_tensor(out=slot, in0=slot, scalar=gain_f[:, sl(g)], in1=sig[:],
                                               op0=ALU.mult, op1=ALU.mult).then_inc(y_ready, 1)

            def evacuate(t, tp):
                for h in range(2):
                    if h == 0:
                        dve.wait_ge(out_done, t + 1)
                    dve.wait_ge(xb_ready, 2 * t + h + 1)
                    nc.vector.tensor_tensor(xo[:, h, :], out_ps[:, 2 * tp + h, :], xo[:, h, :],
                                            ALU.add).then_inc(evacuated, 1)

            def route_top(t):
                dve.wait_ge(logits_done, t + 1)
                nc.vector.tensor_tensor(lg[:], rt_ps[:, P:P + E], rbg[:], ALU.add).then_inc(lg_ready, 1)
                dve.wait_ge(lg_ready, t + 1)
                nc.vector.memset(gate[:, 0:1], 0.0)
                nc.vector.max(top[:], lg[:]).then_inc(top_ready, 1)
                dve.wait_ge(top_ready, t + 1)
                nc.vector.memset(gate[:, 1:2], 0.0)
                nc.vector.max_index(topi[:], top[:], lg[:]).then_inc(topi_ready, 1)
                dve.wait_ge(topi_ready, t + 1)
                nc.vector.tensor_copy(topf[:], topi[:, 0:2]).then_inc(chain, 1)

            def route_weights(t, tp):
                CH = 7
                dve.wait_ge(ex_ready, t + 1)
                nc.vector.tensor_scalar(pr[:, 1:2], pr[:, 0:1], 1.0, None, ALU.add).then_inc(chain, 1)
                dve.wait_ge(chain, CH * t + 2)
                nc.vector.reciprocal(pr[:, 2:3], pr[:, 1:2]).then_inc(chain, 1)
                dve.wait_ge(chain, CH * t + 3)
                nc.vector.tensor_tensor(pr[:, 3:4], pr[:, 0:1], pr[:, 2:3], ALU.mult).then_inc(chain, 1)
                nc.vector.tensor_scalar(coef[:, 0, :], iota_sb[:], topf[:, 0:1], pr[:, 2:3],
                                        ALU.is_equal, ALU.mult).then_inc(chain, 1)
                dve.wait_ge(chain, CH * t + 5)
                nc.vector.tensor_scalar(coef[:, 1, :], iota_sb[:], topf[:, 1:2], pr[:, 3:4],
                                        ALU.is_equal, ALU.mult).then_inc(chain, 1)
                dve.wait_ge(chain, CH * t + 6)
                nc.vector.tensor_tensor(coef[:, 2, :], coef[:, 0, :], coef[:, 1, :], ALU.add).then_inc(chain, 1)
                dve.wait_ge(chain, CH * t + 7)
                nc.vector.tensor_tensor(wx[:].rearrange("p (e r) -> p e r", e=E),
                                        small_ps[:, tp, 0:ER].rearrange("p (e r) -> p e r", e=E),
                                        coef[:, 2, :].unsqueeze(2).to_broadcast([P, E, ER // E]),
                                        ALU.mult).then_inc(wx_ready, 1)

            def step(g, par, head=True, fin=True, ev=True, route=True, hid=True, own_p1=False, first=False):
                t = g - LAG
                if head:
                    dve.wait_ge(e1_ready, g + 1)
                    nc.vector.tensor_scalar(den[:], den[:], EXP30, delta_f[:, sl(g)],
                                            ALU.min, ALU.mult).then_inc(e1_scaled, 1)
                if head and own_p1:
                    dve.wait_ge(e1_scaled, g + 1)
                    if not first:
                        dve.wait_ge(n_ready, g)
                    nc.vector.tensor_tensor(num[:], den[:], kv[:, par, :], ALU.mult).then_inc(p1_ready, 1)
                if ev:
                    evacuate(t - 2, 1 - par)
                if fin and not own_p1:
                    tail(g - 1, 1 - par)
                if head:
                    dve.wait_ge(p1_ready, g + 1)
                    nc.vector.tensor_tensor_scan(den[:], decay(g, T), den[:], 0.0,
                                                 ALU.mult, ALU.add).then_inc(den_fwd, 1)
                if hid:
                    dve.wait_ge(small_done, t + 1)
                    nc.vector.tensor_tensor(hs, small_ps[:, 1 - par, ER:SM], rb1_sb[:],
                                            ALU.add).then_inc(hs_ready, 1)
                if route:
                    route_top(t - 1)
                if head:
                    dve.wait_ge(e2_ready, g + 1)
                    nc.vector.scalar_tensor_tensor(out=kv[:, par, :], in0=eu[:, par, :], scalar=EXP30,
                                                   in1=kv[:, par, :], op0=ALU.min,
                                                   op1=ALU.mult).then_inc(p2_ready, 1)
                if route:
                    route_weights(t - 1, par)
                if head:
                    nc.vector.tensor_tensor_scan(num[:], decay(g, T), num[:], 0.0,
                                                 ALU.mult, ALU.add).then_inc(num_fwd, 1)
                if fin and own_p1:
                    tail(g - 1, 1 - par)
                if head:
                    dve.wait_ge(den_fwd, g + 1)
                    inverse_scale_last(den, g, den_last)
                if hid:
                    dve.wait_ge(hg_ready, t + 1)
                    nc.vector.tensor_tensor(hs, hs, hg[:], ALU.mult).then_inc(h_ready, 1)
                if route:
                    dve.wait_ge(wt_hi_ready, t)
                    nc.vector.tensor_tensor(wt_lo[:, :, :], rt_ps[:, ER:2 * ER].rearrange("p (a t) -> p a t", a=2),
                                            wt_hi[:, :, :].bitcast(fp32), ALU.subtract).then_inc(wt_lo_ready, 1)
                if head:
                    dve.wait_ge(num_fwd, g + 1)
                    inverse_scale_last(num, g, num_last)
                    dve.wait_ge(den_last, g + 1)
                    nc.vector.tensor_tensor_scan(rev(den), decay(g, T - 1), rev(den),
                                                 den[:, T - 1:T], ALU.mult, ALU.add).then_inc(den_bwd, 1)
                    dve.wait_ge(den_bwd, g + 1)
                    nc.vector.scalar_tensor_tensor(out=eu[:, par, :], in0=eu[:, par, :], scalar=EXP30,
                                                   in1=den[:], op0=ALU.min,
                                                   op1=ALU.add).then_inc(den_ready, 1)
                    dve.wait_ge(num_last, g + 1)
                    nc.vector.tensor_tensor_scan(rev(num), decay(g, T - 1), rev(num),
                                                 num[:, T - 1:T], ALU.mult, ALU.add).then_inc(num_bwd, 1)

            step(0, 0, fin=False, ev=False, route=False, hid=False, own_p1=True, first=True)
            with dve.Fori(1, CB - 2, 2) as g:
                step(g, 1, ev=False, route=False, hid=False, own_p1=True)
                step(g + 1, 0, ev=False, route=False, hid=False, own_p1=True)
            step(CB - 1, 1, ev=False, route=False, hid=False, own_p1=True)
            dve.wait_ge(late_in, 16 * LATE)
            nc.vector.tensor_tensor(rbg[:], rb2_sb[:], gates_sb[:], ALU.add).then_inc(rbg_ready, 1)
            step(LAG - 1, 0, ev=False, route=False, hid=False)
            step(LAG, 1, ev=False, route=False)
            dve.wait_ge(rbg_ready, 1)
            step(LAG + 1, 0, ev=False)
            with dve.Fori(LAG + 2, UNITS - 2, 2) as g:
                step(g, 1)
                step(g + 1, 0)
            step(UNITS - 1, 1)
            step(UNITS, 0, head=False)
            with dve.Fori(UNITS + 1, UNITS + CB, 2) as g:
                step(g, 1, head=False, fin=False)
                step(g + 1, 0, head=False, fin=False)
            step(UNITS + LAG, 1, head=False, fin=False, hid=False)
            evacuate(TILES - 1, 1)

        @block.tensor
        def _(pe):
            def three(out_ap, lh, ll, rh, rl, start, stop):
                nc.tensor.matmul(out_ap, lh, rh, start=start, stop=False)
                nc.tensor.matmul(out_ap, lh, rl, start=False, stop=False)
                return nc.tensor.matmul(out_ap, ll, rh, start=False, stop=stop)

            def small(t, par, free=True):
                pe.wait_ge(lo_ready, t + 1)
                if free:
                    pe.wait_ge(wx_ready, t - 1)
                for kc in range(CB):
                    c = slice(kc * WC + D, (kc + 1) * WC)
                    last = three(small_ps[:, par, 0:SM], y_hi[:, par, kc, :], y_lo[:, par, kc, :],
                                 w_hi[:, c], w_lo[:, c], kc == 0, kc == CB - 1)
                last.then_inc(small_done, 1)

            def main(t, par, kc):
                for h in range(2):
                    c = slice(kc * WC + h * HALF, kc * WC + (h + 1) * HALF)
                    last = three(out_ps[:, 2 * par + h, :], y_hi[:, par, kc, :], y_lo[:, par, kc, :],
                                 w_hi[:, c], w_lo[:, c], kc == 0, False)
                if kc == CB - 1:
                    last.then_inc(split_used, 1)

            def hidden_transpose(t):
                pe.wait_ge(h_ready, t + 1)
                nc.tensor.transpose(rt_ps[:, 0:P], hs_wide[:], ident_sb[:]).then_inc(ht_done, 1)

            def logits(t):
                pe.wait_ge(ht_ready, t + 1)
                nc.tensor.matmul(rt_ps[:, P:P + E], ht[:], rw2_sb[:], start=True, stop=True).then_inc(logits_done, 1)

            def weighted_transpose(t):
                pe.wait_ge(wx_ready, t + 1)
                for a in range(2):
                    last = nc.tensor.transpose(rt_ps[:, ER + a * P:ER + (a + 1) * P], wx[:, a * P:(a + 1) * P],
                                               ident_sb[:])
                last.then_inc(wt_done, 1)

            def expert(t, par):
                pe.wait_ge(wt_lo_ready, t + 1)
                for h in range(2):
                    for a in range(2):
                        c0 = CB * WC + a * D + h * HALF
                        last = three(out_ps[:, 2 * par + h, :], wt_hi[:, a, :], wt_lo[:, a, :],
                                     w_hi[:, c0:c0 + HALF], w_lo[:, c0:c0 + HALF], False, a == 1)
                last.then_inc(out_done, 1)

            def step(t, par, route=True, free=True):
                small(t, par, free)
                if route:
                    logits(t - 1)
                if free:
                    pe.wait_ge(evacuated, 2 * (t - 1))
                for kc in range(0, 4):
                    main(t, par, kc)
                if route:
                    weighted_transpose(t - 1)
                for kc in range(4, 6):
                    main(t, par, kc)
                if route:
                    expert(t - 1, 1 - par)
                hidden_transpose(t)
                for kc in range(6, CB):
                    main(t, par, kc)

            pe.wait_ge(w_lo_ready, CHUNKS)
            pe.wait_ge(late_in, 16 * LATE)
            step(0, 0, route=False, free=False)
            step(1, 1, free=False)
            with pe.Fori(2, TILES - 1, 2) as t:
                step(t, 0)
                step(t + 1, 1)
            logits(TILES - 1)
            weighted_transpose(TILES - 1)
            expert(TILES - 1, 1)


def kernel(x, fside_BxSxS_0, cond_512, L0_cond_w, L0_cond_u, L0_ffn_W, L0_ffn_bias, L0_ffn_rw1, L0_ffn_rb1,
           L0_ffn_rw2, L0_ffn_rb2, L0_ffn_A, L0_ffn_B, L0_ffn_gates):
    import concourse.bacc as bacc
    from concourse.bass_utils import run_bass_kernel_spmd

    P = 128
    x = np.asarray(x)
    f = np.asarray(fside_BxSxS_0)
    nb, t, c = x.shape
    cb = c // P
    e, r, _ = L0_ffn_A.shape
    er = e * r
    hid = L0_ffn_rw1.shape[0]
    first = np.concatenate([np.asarray(L0_ffn_W).T, np.asarray(L0_ffn_A).reshape(er, c).T,
                            np.asarray(L0_ffn_rw1).T], axis=1)
    first = first.reshape(cb, P, -1).transpose(1, 0, 2).reshape(P, -1)
    second = np.asarray(L0_ffn_B).transpose(0, 2, 1).reshape(er // P, P, c).transpose(1, 0, 2).reshape(P, -1)
    arrays = {
        "x_cm": x.transpose(0, 2, 1).reshape(nb * cb, P, t),
        "x_tm": x.reshape(nb * t // P, P, c),
        "f_cm": f.transpose(0, 2, 1).reshape(nb * cb, P, t),
        "cond": np.asarray(cond_512),
        "w": np.asarray(L0_cond_w).reshape(cb, P).T,
        "u": np.asarray(L0_cond_u).reshape(cb, P).T,
        "weights": np.concatenate([first, second], axis=1),
        "bias": np.asarray(L0_ffn_bias),
        "rb1": np.asarray(L0_ffn_rb1),
        "rw2": np.asarray(L0_ffn_rw2)[:e].T,
        "rb2": np.asarray(L0_ffn_rb2)[:e],
        "gates": np.asarray(L0_ffn_gates),
        "ident": np.eye(P, dtype=np.float32),
        "iota": np.arange(e, dtype=np.float32),
    }
    arrays = {name: np.ascontiguousarray(a) for name, a in arrays.items()}
    nc = bacc.Bacc("TRN2", target_bir_lowering=False, num_devices=1, dynamic_dma_scratch_size=1024)
    args = [nc.dram_tensor(name, a.shape, mybir.dt.from_np(a.dtype), kind="ExternalInput").ap()
            for name, a in arrays.items()]
    out = nc.dram_tensor("out", (nb * t // P, P, c), mybir.dt.float32, kind="ExternalOutput").ap()
    bidirectional_decay_mix_with_routed_lora(nc, *args, out)
    result = run_bass_kernel_spmd(nc, [arrays], core_ids=[0])
    return result.results[0]["out"].reshape(nb, t, c)
```

```python
import numpy as np
import concourse.bass as bass
from concourse import mybir
from contextlib import ExitStack


def bidirectional_decay_mix_with_routed_lora(nc, x_cm, x_tm, f_cm, cond, w, u, weights, bias, rb1, rw2, rb2, gates,
                                             ident, iota, out):
    fp32, fp32r, u32 = mybir.dt.float32, mybir.dt.float32r, mybir.dt.uint32
    ALU = mybir.AluOpType
    ACT = mybir.ActivationFunctionType
    AX = mybir.AxisListType

    P = 128
    UNITS, _, T = f_cm.shape
    TILES, _, D = x_tm.shape
    NB, TD = cond.shape
    CB = UNITS // NB
    LAG = CB + 1
    E = gates.shape[-1]
    HID = rb1.shape[-1]
    ER = 2 * P
    SM = ER + HID
    WC = D + SM
    HALF = D // 2
    CHUNKS = 5
    CHUNK = weights.shape[1] // CHUNKS
    STAGE = 3 * T
    EXP30 = float(np.float32(np.exp(30.0)))
    DEN_MIN_INV = 1e8

    with ExitStack() as ctx:
        def sb(name, shape, dt=fp32):
            return ctx.enter_context(nc.sbuf_tensor(name, shape, dt))

        def pb(name, shape, dt=fp32):
            return ctx.enter_context(nc.psum_tensor(name, shape, dt))

        def sem(name):
            return ctx.enter_context(nc.semaphore(name))

        w_hi = sb("w_hi", [P, weights.shape[1]], fp32r)
        w_lo = sb("w_lo", [P, weights.shape[1]], fp32r)
        y = sb("y", [P, 2 * CB, T])
        y_hi = sb("y_hi", [P, 2, CB, P], fp32r)
        y_lo = sb("y_lo", [P, 2, CB, P], fp32r)
        kv = sb("kv", [P, 2, T])
        den = sb("den", [P, T])
        num = sb("num", [P, T])
        eu = sb("eu", [P, 2, T])
        sig = sb("sig", [P, T])
        xo = sb("xo", [P, 2, HALF])
        bias_sb = sb("bias_sb", [P, D])
        wx = sb("wx", [P, ER])
        wt_hi = sb("wt_hi", [P, 2, P], fp32r)
        wt_lo = sb("wt_lo", [P, 2, P], fp32r)
        ident_sb = sb("ident_sb", [P, P])
        ht = sb("ht", [HID, P])
        hs_wide = sb("hs_wide", [P, P])
        hs = hs_wide[:, 0:HID]
        gate = sb("gate", [P, 2])

        hg = sb("hg", [P, HID])
        rb1_sb = sb("rb1_sb", [P, HID])
        rw2_sb = sb("rw2_sb", [HID, E])
        rb2_sb = sb("rb2_sb", [P, E])
        gates_sb = sb("gates_sb", [P, E])
        rbg = sb("rbg", [P, E])
        iota_sb = sb("iota_sb", [P, E])
        lg = sb("lg", [P, E])
        coef = sb("coef", [P, 3, E])
        top = sb("top", [P, 8])
        topi = sb("topi", [P, 8], u32)
        topf = sb("topf", [P, 2])
        pr = sb("pr", [P, 4])
        w_sb = sb("w_sb", [P, CB])
        u_sb = sb("u_sb", [P, CB])
        u_g = sb("u_g", [P, NB, CB])
        delta_g = sb("delta_g", [P, NB, CB])
        rdelta_g = sb("rdelta_g", [P, NB, CB])
        log_gain_g = sb("log_gain_g", [P, NB, CB])
        limit_g = sb("limit_g", [P, NB, CB])
        tiny = sb("tiny", [P, 1])

        out_ps = pb("out_ps", [P, 4, HALF])
        small_ps = pb("small_ps", [P, 2, 512])
        rt_ps = pb("rt_ps", [P, 512])
        d_ps = pb("d_ps", [P, 512])

        w_raw = y[:, :, :].rearrange("p s t -> p (s t)")[:, STAGE:STAGE + weights.shape[1]]
        cond_sb = y[:, 1, :]
        dd = y[:, 2, 0:2 * UNITS].rearrange("p (a b c) -> p a b c", a=2, b=NB)
        d_g = y[:, 2, 2 * UNITS:3 * UNITS].rearrange("p (b c) -> p b c", b=NB)
        tf = y[:, 2, 3 * UNITS:3 * UNITS + 5 * NB].rearrange("p (a b) -> p a b", a=5)
        flat = lambda t: t[:, :, :].rearrange("p b c -> p (b c)")
        u_f, delta_f, rdelta_f, log_gain_f, limit_f = (flat(u_g), flat(delta_g), flat(rdelta_g), flat(log_gain_g),
                                                       flat(limit_g))
        num_of = [num, xo[:, :, :].rearrange("p h c -> p (h c)")]

        late = [(rb1_sb[:], rb1.partition_broadcast(P)), (rb2_sb[:], rb2.partition_broadcast(P)),
                (gates_sb[:], gates.partition_broadcast(P)), (bias_sb[:], bias.partition_broadcast(P)),
                (iota_sb[:], iota.partition_broadcast(P)), (ident_sb[:], ident), (rw2_sb[:], rw2)]
        LATE = len(late)

        params_in = sem("params_in")
        late_in = sem("late_in")
        w_in = sem("w_in")
        k_in = [sem("k_in0"), sem("k_in1")]
        r_in = sem("r_in")
        x_in = [sem("x_in0"), sem("x_in1")]
        out_stored = [sem("out_stored0"), sem("out_stored1")]
        setup_act = sem("setup_act")
        setup_dve = sem("setup_dve")
        rbg_ready = sem("rbg_ready")
        gain_ready = sem("gain_ready")
        factors_ready = sem("factors_ready")
        gains_ready = sem("gains_ready")
        w_hi_ready = sem("w_hi_ready")
        w_lo_ready = sem("w_lo_ready")
        e1_ready = sem("e1_ready")
        e2_ready = sem("e2_ready")
        e1_scaled = sem("e1_scaled")
        p1_ready = sem("p1_ready")
        p2_ready = sem("p2_ready")
        den_fwd = sem("den_fwd")
        num_fwd = sem("num_fwd")
        den_last = sem("den_last")
        num_last = sem("num_last")
        den_bwd = sem("den_bwd")
        num_bwd = sem("num_bwd")
        den_ready = sem("den_ready")
        n_ready = sem("n_ready")
        log_ready = sem("log_ready")
        q_ready = sem("q_ready")
        ratio_ready = sem("ratio_ready")
        sig_ready = sem("sig_ready")
        y_ready = sem("y_ready")
        hi_ready = sem("hi_ready")
        lo_ready = sem("lo_ready")
        split_used = sem("split_used")
        small_done = sem("small_done")
        hs_ready = sem("hs_ready")
        hg_ready = sem("hg_ready")
        h_ready = sem("h_ready")
        ht_done = sem("ht_done")
        ht_ready = sem("ht_ready")
        logits_done = sem("logits_done")
        lg_ready = sem("lg_ready")
        top_ready = sem("top_ready")
        topi_ready = sem("topi_ready")
        ex_ready = sem("ex_ready")
        chain = sem("chain")
        wx_ready = sem("wx_ready")
        wt_done = sem("wt_done")
        wt_hi_ready = sem("wt_hi_ready")
        wt_lo_ready = sem("wt_lo_ready")
        out_done = sem("out_done")
        xb_ready = sem("xb_ready")
        evacuated = sem("evacuated")

        def sl(i):
            return bass.ds(i, 1)

        def row(t, i):
            return t[:, sl(i), :].rearrange("p a t -> p (a t)")

        def rev(a):
            return a[:, T - 2::-1]

        def tile_of_y(t):
            base = (t // CB) % 2 * CB
            return y[:, bass.ds(base, CB), bass.ds(t % CB * P, P)]

        block = ctx.enter_context(nc.Block())

        @block.sync
        def _(sp):
            sp.dma_start(cond_sb, cond.rearrange("b t -> (b t)").partition_broadcast(P)).then_inc(params_in, 16)
            sp.dma_start(kv[:, 0, :], f_cm[0]).then_inc(k_in[0], 16)
            sp.dma_start(w_sb[:], w).then_inc(params_in, 16)
            sp.dma_start(u_sb[:], u).then_inc(params_in, 16)
            sp.dma_start(kv[:, 1, :], f_cm[1]).then_inc(k_in[1], 16)
            sp.dma_start(sig[:], x_cm[0]).then_inc(r_in, 16)
            for dst, src in late:
                sp.dma_start(dst, src).then_inc(late_in, 16)
            for n in range(CHUNKS):
                sp.dma_start(w_raw[:, n * CHUNK:(n + 1) * CHUNK],
                             weights[:, n * CHUNK:(n + 1) * CHUNK]).then_inc(w_in, 16)

            def load_k(g, par):
                sp.wait_ge(n_ready, g - 1)
                sp.dma_start(kv[:, par, :], f_cm[sl(g)].rearrange("a p t -> (a p) t")).then_inc(k_in[par], 16)

            def load_r(g):
                sp.wait_ge(y_ready, g)
                sp.dma_start(sig[:], x_cm[sl(g)].rearrange("a p t -> (a p) t")).then_inc(r_in, 16)

            def store(t):
                for h in range(2):
                    sp.wait_ge(evacuated, 2 * t + h + 1)
                    sp.dma_start(out[sl(t), :, h * HALF:(h + 1) * HALF].rearrange("a p c -> (a p) c"),
                                 xo[:, h, :]).then_inc(out_stored[h], 16)

            def load_x(t, first=False):
                for h in range(2):
                    if first:
                        sp.wait_ge(n_ready, CB)
                    else:
                        sp.wait_ge(out_stored[h], 16 * t)
                    sp.dma_start(xo[:, h, :],
                                 x_tm[sl(t), :, h * HALF:(h + 1) * HALF].rearrange("a p c -> (a p) c")
                                 ).then_inc(x_in[h], 16)

            def step(g, par, k=True, r=True, st=True, lx=True, first=False):
                t = g - LAG
                if k:
                    load_k(g + 1, 1 - par)
                if st:
                    store(t - 2)
                if r:
                    load_r(g)
                if lx:
                    load_x(t - 1, first)

            with sp.Fori(1, LAG - 1, 2) as g:
                step(g, 1, st=False, lx=False)
                step(g + 1, 0, st=False, lx=False)
            step(LAG, 1, st=False, lx=False)
            step(LAG + 1, 0, st=False, first=True)
            with sp.Fori(LAG + 2, UNITS - 2, 2) as g:
                step(g, 1)
                step(g + 1, 0)
            step(UNITS - 1, 1, k=False)
            with sp.Fori(UNITS, UNITS + LAG + 1) as g:
                step(g, 0, k=False, r=False)
            store(TILES - 1)
            for h in range(2):
                sp.wait_ge(out_stored[h], 16 * TILES)

        @block.scalar
        def _(act):
            def exp_k(g, par, first=False):
                act.wait_ge(k_in[par], 16 * (g // 2 + 1))
                if not first:
                    act.wait_ge(den_ready, g)
                nc.scalar.activation(den[:], kv[:, par, :], ACT.Exp).then_inc(e1_ready, 1)

            nc.scalar.preload_act_table_set("natural_log_exp_and_others")
            exp_k(0, 0, first=True)
            act.wait_ge(params_in, 48)
            nc.scalar.activation(w_sb[:], w_sb[:], ACT.Exp).then_inc(setup_act, 1)
            act.wait_ge(setup_act, 1)
            nc.scalar.activation(w_sb[:], w_sb[:], ACT.Exp, scale=-1.0).then_inc(setup_act, 1)
            act.wait_ge(setup_dve, 1)
            nc.scalar.activation(tf[:, 1, :], tf[:, 0, :], ACT.Sigmoid).then_inc(setup_act, 1)

            def exp_uk(g, par, first=False):
                act.wait_ge(k_in[par], 16 * (g // 2 + 1))
                if not first:
                    act.wait_ge(ratio_ready, g - 1)
                nc.scalar.activation(eu[:, par, :], kv[:, par, :], ACT.Exp,
                                     bias=u_f[:, sl(g)]).then_inc(e2_ready, 1)

            def inverse(g, par):
                act.wait_ge(den_ready, g + 1)
                nc.scalar.activation(eu[:, par, :], eu[:, par, :], ACT.Ln, bias=tiny[:]).then_inc(log_ready, 1)
                act.wait_ge(log_ready, g + 1)
                nc.scalar.activation(eu[:, par, :], eu[:, par, :], ACT.Exp, bias=log_gain_f[:, sl(g)],
                                     scale=-1.0).then_inc(q_ready, 1)

            def weights_hi(n):
                nc.scalar.activation(w_hi[:, bass.ds(n * CHUNK, CHUNK)], w_raw[:, bass.ds(n * CHUNK, CHUNK)],
                                     ACT.Copy).then_inc(w_hi_ready, 1)

            def split_hi(t, par, first=False):
                act.wait_ge(y_ready, (t // CB + 1) * CB)
                if not first:
                    act.wait_ge(split_used, t - 1)
                nc.scalar.activation(y_hi[:, par, :, :], tile_of_y(t), ACT.Copy).then_inc(hi_ready, 1)

            def sigmoid_r(g):
                act.wait_ge(r_in, 16 * (g + 1))
                nc.scalar.activation(sig[:], sig[:], ACT.Sigmoid).then_inc(sig_ready, 1)

            def step(g, par, ek=True, inv=True, ex=True, hi=True, first_hi=False, route=True, s=True, s_prev=False,
                     hid=True, weights=None):
                t = g - LAG
                if ek:
                    exp_k(g, par)
                if route:
                    act.wait_ge(ht_done, t)
                    nc.scalar.copy(ht[:], rt_ps[0:HID, 0:P]).then_inc(ht_ready, 1)
                if inv:
                    inverse(g - 1, 1 - par)
                if s_prev:
                    sigmoid_r(g - 1)
                    nc.scalar.preload_act_table_set("natural_log_exp_and_others")
                if weights is not None:
                    weights_hi(weights)
                if ex:
                    exp_uk(g + 1, 1 - par)
                if hi:
                    split_hi(t + 1, par, first_hi)
                if route:
                    act.wait_ge(top_ready, t)
                    nc.scalar.activation(pr[:, 0:1], top[:, 0:1], ACT.Exp, bias=top[:, 1:2],
                                         scale=-1.0).then_inc(ex_ready, 1)
                if hid:
                    act.wait_ge(hs_ready, t + 1)
                    nc.scalar.activation(hg[:], hs, ACT.Sigmoid).then_inc(hg_ready, 1)
                if route:
                    act.wait_ge(wt_done, t)
                    nc.scalar.copy(wt_hi[:, :, :], rt_ps[:, ER:2 * ER].rearrange("p (a t) -> p a t", a=2)
                                   ).then_inc(wt_hi_ready, 1)
                if s:
                    sigmoid_r(g)
                if s or hid:
                    nc.scalar.preload_act_table_set("natural_log_exp_and_others")

            nc.scalar.preload_act_table_set("natural_log_exp_and_others")
            act.wait_ge(gain_ready, 1)
            nc.scalar.activation(tf[:, 4, :], tf[:, 3, :], ACT.Ln).then_inc(setup_act, 1)
            act.wait_ge(setup_dve, 3)
            exp_uk(0, 0, first=True)
            exp_uk(1, 1, first=True)
            act.wait_ge(gains_ready, 2)
            step(1, 1, hi=False, route=False, s=False, s_prev=True, hid=False)
            act.wait_ge(w_in, 16 * CHUNKS)
            step(2, 0, hi=False, route=False, s=False, s_prev=True, hid=False, weights=0)
            with act.Fori(3, 3 + CHUNKS - 2, 2) as g:
                step(g, 1, hi=False, route=False, s=False, s_prev=True, hid=False, weights=g - 2)
                step(g + 1, 0, hi=False, route=False, s=False, s_prev=True, hid=False, weights=g - 1)
            step(CB - 1, 1, hi=False, route=False, s=False, s_prev=True, hid=False)
            step(LAG - 1, 0, first_hi=True, route=False, s_prev=True, hid=False)
            step(LAG, 1, first_hi=True, route=False)
            with act.Fori(LAG + 1, UNITS - 3, 2) as g:
                step(g, 0)
                step(g + 1, 1)
            step(UNITS - 2, 0)
            step(UNITS - 1, 1, ex=False)
            step(UNITS, 0, ek=False, ex=False, s=False)
            with act.Fori(UNITS + 1, UNITS + CB - 2, 2) as g:
                step(g, 1, ek=False, inv=False, ex=False, s=False)
                step(g + 1, 0, ek=False, inv=False, ex=False, s=False)
            step(UNITS + CB - 1, 1, ek=False, inv=False, ex=False, s=False)
            step(UNITS + CB, 0, ek=False, inv=False, ex=False, hi=False, s=False)
            step(UNITS + LAG, 1, ek=False, inv=False, ex=False, hi=False, s=False, hid=False)

        @block.gpsimd
        def _(pool):
            def weights_lo(n):
                pool.wait_ge(w_hi_ready, n + 1)
                c = bass.ds(n * CHUNK, CHUNK)
                nc.gpsimd.tensor_tensor(w_lo[:, c], w_raw[:, c], w_hi[:, c].bitcast(fp32),
                                        ALU.subtract).then_inc(w_lo_ready, 1)

            def gate_y(g):
                pool.wait_ge(sig_ready, g + 1)
                pool.wait_ge(ratio_ready, g + 1)
                slot = row(y, (g + 2 * CB) % (2 * CB))
                nc.gpsimd.tensor_tensor(slot, slot, sig[:], ALU.mult).then_inc(y_ready, 1)

            def step(g, par, lo=True, mix=True, x=True, p1=True, fin=True, weights=None, pieces=True):
                t = g - LAG
                num = num_of[0] if p1 else num_of[par]
                if mix and p1:
                    pool.wait_ge(n_ready, g)
                    pool.wait_ge(e1_scaled, g + 1)
                    nc.gpsimd.tensor_tensor(num[:], den[:], kv[:, par, :], ALU.mult).then_inc(p1_ready, 1)
                if fin:
                    gate_y(g - 1)
                if lo:
                    pool.wait_ge(hi_ready, t + 2)
                    nc.gpsimd.tensor_tensor(y_lo[:, par, :, :], tile_of_y(t + 1), y_hi[:, par, :, :].bitcast(fp32),
                                            ALU.subtract).then_inc(lo_ready, 1)
                if x:
                    for h in range(2):
                        pool.wait_ge(x_in[h], 16 * t)
                        nc.gpsimd.tensor_tensor(xo[:, h, :], xo[:, h, :], bias_sb[:, h * HALF:(h + 1) * HALF],
                                                ALU.add).then_inc(xb_ready, 1)
                if mix:
                    if not p1 and pieces:
                        pool.wait_ge(w_lo_ready, g - 2)
                    pool.wait_ge(num_bwd, g + 1)
                    pool.wait_ge(p2_ready, g + 1)
                    nc.gpsimd.tensor_tensor(row(y, g % (2 * CB)), num[:], kv[:, par, :],
                                            ALU.add).then_inc(n_ready, 1)
                if weights is not None:
                    weights_lo(weights)

            step(0, 0, lo=False, x=False, p1=False, fin=False, pieces=False)
            step(1, 1, lo=False, x=False, p1=False, pieces=False)
            step(2, 0, lo=False, x=False, p1=False, pieces=False, weights=0)
            with pool.Fori(3, 3 + CHUNKS - 2, 2) as g:
                step(g, 1, lo=False, x=False, p1=False, weights=g - 2)
                step(g + 1, 0, lo=False, x=False, p1=False, weights=g - 1)
            gate_y(CB - 2)
            pool.wait_ge(late_in, 16 * LATE)
            step(LAG - 1, 0, lo=False, x=False, fin=False)
            step(LAG, 1, x=False)
            with pool.Fori(LAG + 1, UNITS - 1, 2) as g:
                step(g, 0)
                step(g + 1, 1)
            step(UNITS, 0, mix=False)
            with pool.Fori(UNITS + 1, UNITS + CB - 2, 2) as g:
                step(g, 1, mix=False, fin=False)
                step(g + 1, 0, mix=False, fin=False)
            step(UNITS + CB - 1, 1, mix=False, fin=False)
            step(UNITS + CB, 0, lo=False, mix=False, fin=False)
            step(UNITS + LAG, 1, lo=False, mix=False, fin=False)

        @block.vector
        def _(dve):
            count = [0]

            def link(ins):
                count[0] += 1
                ins.then_inc(setup_dve, 1)
                dve.wait_ge(setup_dve, count[0])

            dve.wait_ge(params_in, 48)
            link(nc.vector.reduce_sum(tf[:, 0, :], cond_sb.rearrange("p (b t) -> p b t", b=NB), AX.X))
            over_cb = lambda a: a.unsqueeze(2).to_broadcast([P, NB, CB])
            over_nb = lambda a: a.unsqueeze(1).to_broadcast([P, NB, CB])
            link(nc.vector.tensor_copy(u_g[:, :, :], over_nb(u_sb[:, :])))
            link(nc.vector.memset(tiny[:], 1e-19))
            link(nc.vector.memset(hs_wide[:], 0.0))
            link(nc.vector.memset(coef[:, 2, 0:1], 0.0))
            dve.wait_ge(setup_act, 3)
            link(nc.vector.tensor_scalar(tf[:, 2, :], tf[:, 1, :], 0.5, 0.5, ALU.mult, ALU.add))
            link(nc.vector.tensor_tensor(d_g[:, :, :], over_nb(w_sb[:, :]), over_cb(tf[:, 2, :]), ALU.mult))
            nc.vector.tensor_scalar(tf[:, 3, :], tf[:, 1, :], 0.2, 0.8, ALU.mult, ALU.add).then_inc(gain_ready, 1)
            nc.vector.tensor_scalar(dd[:, 0, :, :], d_g[:, :, :], -1.0, 1.0, ALU.mult, ALU.add
                                    ).then_inc(factors_ready, 1)
            nc.vector.tensor_scalar(dd[:, 1, :, :], d_g[:, :, :], 1.0, None, ALU.add).then_inc(factors_ready, 1)
            dve.wait_ge(factors_ready, 2)
            link(nc.vector.tensor_tensor(delta_g[:, :, :], dd[:, 0, :, :], dd[:, 1, :, :], ALU.mult))
            link(nc.vector.tensor_scalar(delta_g[:, :, :], delta_g[:, :, :], 1e-12, None, ALU.max))
            link(nc.vector.tensor_copy(d_ps[:, 0:UNITS], y[:, 2, 2 * UNITS:3 * UNITS]))

            def late_setup():
                link(nc.vector.reciprocal(rdelta_g[:, :, :], delta_g[:, :, :]))
                dve.wait_ge(setup_act, 4)
                nc.vector.tensor_scalar(limit_g[:, :, :], over_cb(tf[:, 3, :]), DEN_MIN_INV, None,
                                        ALU.mult).then_inc(gains_ready, 1)
                nc.vector.tensor_copy(log_gain_g[:, :, :], over_cb(tf[:, 4, :])).then_inc(gains_ready, 1)

            def decay(g, n):
                return d_ps[:, sl(g)].to_broadcast([P, n])

            def inverse_scale_last(a, g, done):
                last = a[:, T - 1:T]
                nc.vector.tensor_scalar(last, last, rdelta_f[:, sl(g)], None, ALU.mult).then_inc(done, 1)

            def ratio(g, par):
                slot = row(y, g % (2 * CB))
                dve.wait_ge(q_ready, g + 1)
                dve.wait_ge(n_ready, g + 1)
                nc.vector.scalar_tensor_tensor(out=slot, in0=eu[:, par, :], scalar=limit_f[:, sl(g)], in1=slot,
                                               op0=ALU.min, op1=ALU.mult).then_inc(ratio_ready, 1)

            def evacuate(t, tp):
                for h in range(2):
                    if h == 0:
                        dve.wait_ge(out_done, t + 1)
                    dve.wait_ge(xb_ready, 2 * t + h + 1)
                    nc.vector.tensor_tensor(xo[:, h, :], out_ps[:, 2 * tp + h, :], xo[:, h, :],
                                            ALU.add).then_inc(evacuated, 1)

            def route_top(t):
                dve.wait_ge(logits_done, t + 1)
                nc.vector.tensor_tensor(lg[:], rt_ps[:, P:P + E], rbg[:], ALU.add).then_inc(lg_ready, 1)
                dve.wait_ge(lg_ready, t + 1)
                nc.vector.memset(gate[:, 0:1], 0.0)
                nc.vector.max(top[:], lg[:]).then_inc(top_ready, 1)
                dve.wait_ge(top_ready, t + 1)
                nc.vector.memset(gate[:, 1:2], 0.0)
                nc.vector.max_index(topi[:], top[:], lg[:]).then_inc(topi_ready, 1)
                dve.wait_ge(topi_ready, t + 1)
                nc.vector.tensor_copy(topf[:], topi[:, 0:2]).then_inc(chain, 1)

            def route_weights(t, tp):
                CH = 7
                dve.wait_ge(ex_ready, t + 1)
                nc.vector.tensor_scalar(pr[:, 1:2], pr[:, 0:1], 1.0, None, ALU.add).then_inc(chain, 1)
                dve.wait_ge(chain, CH * t + 2)
                nc.vector.reciprocal(pr[:, 2:3], pr[:, 1:2]).then_inc(chain, 1)
                dve.wait_ge(chain, CH * t + 3)
                nc.vector.tensor_tensor(pr[:, 3:4], pr[:, 0:1], pr[:, 2:3], ALU.mult).then_inc(chain, 1)
                nc.vector.tensor_scalar(coef[:, 0, :], iota_sb[:], topf[:, 0:1], pr[:, 2:3],
                                        ALU.is_equal, ALU.mult).then_inc(chain, 1)
                dve.wait_ge(chain, CH * t + 5)
                nc.vector.tensor_scalar(coef[:, 1, :], iota_sb[:], topf[:, 1:2], pr[:, 3:4],
                                        ALU.is_equal, ALU.mult).then_inc(chain, 1)
                dve.wait_ge(chain, CH * t + 6)
                nc.vector.tensor_tensor(coef[:, 2, :], coef[:, 0, :], coef[:, 1, :], ALU.add).then_inc(chain, 1)
                dve.wait_ge(chain, CH * t + 7)
                nc.vector.tensor_tensor(wx[:].rearrange("p (e r) -> p e r", e=E),
                                        small_ps[:, tp, 0:ER].rearrange("p (e r) -> p e r", e=E),
                                        coef[:, 2, :].unsqueeze(2).to_broadcast([P, E, ER // E]),
                                        ALU.mult).then_inc(wx_ready, 1)

            def step(g, par, head=True, fin=True, ev=True, route=True, hid=True, own_p1=False, first=False,
                     first_tile=False, setup=False):
                t = g - LAG
                num = num_of[par] if own_p1 else num_of[0]
                if head:
                    dve.wait_ge(e1_ready, g + 1)
                    nc.vector.tensor_scalar(den[:], den[:], EXP30, delta_f[:, sl(g)],
                                            ALU.min, ALU.mult).then_inc(e1_scaled, 1)
                if head and own_p1:
                    dve.wait_ge(e1_scaled, g + 1)
                    if not first:
                        dve.wait_ge(n_ready, g - 1)
                    nc.vector.tensor_tensor(num[:], den[:], kv[:, par, :], ALU.mult).then_inc(p1_ready, 1)
                if ev:
                    evacuate(t - 2, 1 - par)
                if fin and not own_p1:
                    ratio(g - 1, 1 - par)
                if first_tile:
                    slot = row(y, CB - 1)
                    dve.wait_ge(ratio_ready, CB)
                    dve.wait_ge(sig_ready, CB)
                    dve.wait_ge(y_ready, CB - 1)
                    nc.vector.tensor_tensor(slot, slot, sig[:], ALU.mult).then_inc(y_ready, 1)
                if head:
                    dve.wait_ge(p1_ready, g + 1)
                    nc.vector.tensor_tensor_scan(den[:], decay(g, T), den[:], 0.0,
                                                 ALU.mult, ALU.add).then_inc(den_fwd, 1)
                if first_tile:
                    dve.wait_ge(hi_ready, 1)
                    nc.vector.tensor_tensor(y_lo[:, 0, :, :], tile_of_y(0), y_hi[:, 0, :, :].bitcast(fp32),
                                            ALU.subtract).then_inc(lo_ready, 1)
                if hid:
                    dve.wait_ge(small_done, t + 1)
                    nc.vector.tensor_tensor(hs, small_ps[:, 1 - par, ER:SM], rb1_sb[:],
                                            ALU.add).then_inc(hs_ready, 1)
                if route:
                    route_top(t - 1)
                if head:
                    dve.wait_ge(e2_ready, g + 1)
                    nc.vector.scalar_tensor_tensor(out=kv[:, par, :], in0=eu[:, par, :], scalar=EXP30,
                                                   in1=kv[:, par, :], op0=ALU.min,
                                                   op1=ALU.mult).then_inc(p2_ready, 1)
                if route:
                    route_weights(t - 1, par)
                if head:
                    nc.vector.tensor_tensor_scan(num[:], decay(g, T), num[:], 0.0,
                                                 ALU.mult, ALU.add).then_inc(num_fwd, 1)
                if fin and own_p1:
                    ratio(g - 1, 1 - par)
                if setup:
                    late_setup()
                if head:
                    dve.wait_ge(den_fwd, g + 1)
                    inverse_scale_last(den, g, den_last)
                if hid:
                    dve.wait_ge(hg_ready, t + 1)
                    nc.vector.tensor_tensor(hs, hs, hg[:], ALU.mult).then_inc(h_ready, 1)
                if route:
                    dve.wait_ge(wt_hi_ready, t)
                    nc.vector.tensor_tensor(wt_lo[:, :, :], rt_ps[:, ER:2 * ER].rearrange("p (a t) -> p a t", a=2),
                                            wt_hi[:, :, :].bitcast(fp32), ALU.subtract).then_inc(wt_lo_ready, 1)
                if head:
                    dve.wait_ge(num_fwd, g + 1)
                    inverse_scale_last(num, g, num_last)
                    dve.wait_ge(den_last, g + 1)
                    nc.vector.tensor_tensor_scan(rev(den), decay(g, T - 1), rev(den),
                                                 den[:, T - 1:T], ALU.mult, ALU.add).then_inc(den_bwd, 1)
                    dve.wait_ge(den_bwd, g + 1)
                    nc.vector.scalar_tensor_tensor(out=eu[:, par, :], in0=eu[:, par, :], scalar=EXP30,
                                                   in1=den[:], op0=ALU.min,
                                                   op1=ALU.add).then_inc(den_ready, 1)
                    dve.wait_ge(num_last, g + 1)
                    nc.vector.tensor_tensor_scan(rev(num), decay(g, T - 1), rev(num),
                                                 num[:, T - 1:T], ALU.mult, ALU.add).then_inc(num_bwd, 1)

            step(0, 0, fin=False, ev=False, route=False, hid=False, own_p1=True, first=True, setup=True)
            step(1, 1, ev=False, route=False, hid=False, own_p1=True, first=True)
            with dve.Fori(2, CB - 1, 2) as g:
                step(g, 0, ev=False, route=False, hid=False, own_p1=True)
                step(g + 1, 1, ev=False, route=False, hid=False, own_p1=True)
            dve.wait_ge(n_ready, CB - 1)
            dve.wait_ge(w_lo_ready, CHUNKS - 1)
            dve.wait_ge(num_bwd, CB)
            nc.vector.tensor_tensor(y[:, CB - 1, :], num_of[1][:, :], kv[:, 1, :], ALU.add).then_inc(n_ready, 1)
            dve.wait_ge(late_in, 16 * LATE)
            nc.vector.tensor_tensor(rbg[:], rb2_sb[:], gates_sb[:], ALU.add).then_inc(rbg_ready, 1)
            step(LAG - 1, 0, ev=False, route=False, hid=False, first_tile=True)
            step(LAG, 1, ev=False, route=False)
            dve.wait_ge(rbg_ready, 1)
            step(LAG + 1, 0, ev=False)
            with dve.Fori(LAG + 2, UNITS - 2, 2) as g:
                step(g, 1)
                step(g + 1, 0)
            step(UNITS - 1, 1)
            step(UNITS, 0, head=False)
            with dve.Fori(UNITS + 1, UNITS + CB, 2) as g:
                step(g, 1, head=False, fin=False)
                step(g + 1, 0, head=False, fin=False)
            step(UNITS + LAG, 1, head=False, fin=False, hid=False)
            evacuate(TILES - 1, 1)

        @block.tensor
        def _(pe):
            def three(out_ap, lh, ll, rh, rl, start, stop):
                nc.tensor.matmul(out_ap, lh, rh, start=start, stop=False)
                nc.tensor.matmul(out_ap, lh, rl, start=False, stop=False)
                return nc.tensor.matmul(out_ap, ll, rh, start=False, stop=stop)

            def small(t, par, free=True):
                pe.wait_ge(lo_ready, t + 1)
                if free:
                    pe.wait_ge(wx_ready, t - 1)
                for kc in range(CB):
                    c = slice(kc * WC + D, (kc + 1) * WC)
                    last = three(small_ps[:, par, 0:SM], y_hi[:, par, kc, :], y_lo[:, par, kc, :],
                                 w_hi[:, c], w_lo[:, c], kc == 0, kc == CB - 1)
                last.then_inc(small_done, 1)

            def main(t, par, kc):
                for h in range(2):
                    c = slice(kc * WC + h * HALF, kc * WC + (h + 1) * HALF)
                    last = three(out_ps[:, 2 * par + h, :], y_hi[:, par, kc, :], y_lo[:, par, kc, :],
                                 w_hi[:, c], w_lo[:, c], kc == 0, False)
                if kc == CB - 1:
                    last.then_inc(split_used, 1)

            def hidden_transpose(t):
                pe.wait_ge(h_ready, t + 1)
                nc.tensor.transpose(rt_ps[:, 0:P], hs_wide[:], ident_sb[:]).then_inc(ht_done, 1)

            def logits(t):
                pe.wait_ge(ht_ready, t + 1)
                nc.tensor.matmul(rt_ps[:, P:P + E], ht[:], rw2_sb[:], start=True, stop=True).then_inc(logits_done, 1)

            def weighted_transpose(t):
                pe.wait_ge(wx_ready, t + 1)
                for a in range(2):
                    last = nc.tensor.transpose(rt_ps[:, ER + a * P:ER + (a + 1) * P], wx[:, a * P:(a + 1) * P],
                                               ident_sb[:])
                last.then_inc(wt_done, 1)

            def expert(t, par):
                pe.wait_ge(wt_lo_ready, t + 1)
                for h in range(2):
                    for a in range(2):
                        c0 = CB * WC + a * D + h * HALF
                        last = three(out_ps[:, 2 * par + h, :], wt_hi[:, a, :], wt_lo[:, a, :],
                                     w_hi[:, c0:c0 + HALF], w_lo[:, c0:c0 + HALF], False, a == 1)
                last.then_inc(out_done, 1)

            def step(t, par, route=True, free=True, before_routing=5, before_expert=7):
                small(t, par, free)
                if route:
                    logits(t - 1)
                if free:
                    pe.wait_ge(evacuated, 2 * (t - 1))
                for kc in range(0, before_routing):
                    main(t, par, kc)
                if route:
                    weighted_transpose(t - 1)
                for kc in range(before_routing, before_expert):
                    main(t, par, kc)
                if route:
                    expert(t - 1, 1 - par)
                hidden_transpose(t)
                for kc in range(before_expert, CB):
                    main(t, par, kc)

            pe.wait_ge(w_lo_ready, CHUNKS)
            pe.wait_ge(late_in, 16 * LATE)
            step(0, 0, route=False, free=False, before_expert=CB)
            step(1, 1, free=False, before_routing=CB - 1, before_expert=CB)
            step(2, 0, before_routing=6)
            with pe.Fori(3, TILES - 2, 2) as t:
                step(t, 1)
                step(t + 1, 0)
            last = TILES - 1
            small(last, 1)
            logits(last - 1)
            pe.wait_ge(evacuated, 2 * (last - 1))
            for kc in range(0, 3):
                main(last, 1, kc)
            weighted_transpose(last - 1)
            main(last, 1, 3)
            expert(last - 1, 0)
            hidden_transpose(last)
            for kc in range(4, 6):
                main(last, 1, kc)
            logits(last)
            for kc in range(6, CB):
                main(last, 1, kc)
            weighted_transpose(last)
            expert(last, 1)


def kernel(x, fside_BxSxS_0, cond_512, L0_cond_w, L0_cond_u, L0_ffn_W, L0_ffn_bias, L0_ffn_rw1, L0_ffn_rb1,
           L0_ffn_rw2, L0_ffn_rb2, L0_ffn_A, L0_ffn_B, L0_ffn_gates):
    import concourse.bacc as bacc
    from concourse.bass_utils import run_bass_kernel_spmd

    P = 128
    x = np.asarray(x)
    f = np.asarray(fside_BxSxS_0)
    nb, t, c = x.shape
    cb = c // P
    e, r, _ = L0_ffn_A.shape
    er = e * r
    hid = L0_ffn_rw1.shape[0]
    first = np.concatenate([np.asarray(L0_ffn_W).T, np.asarray(L0_ffn_A).reshape(er, c).T,
                            np.asarray(L0_ffn_rw1).T], axis=1)
    first = first.reshape(cb, P, -1).transpose(1, 0, 2).reshape(P, -1)
    second = np.asarray(L0_ffn_B).transpose(0, 2, 1).reshape(er // P, P, c).transpose(1, 0, 2).reshape(P, -1)
    arrays = {
        "x_cm": x.transpose(0, 2, 1).reshape(nb * cb, P, t),
        "x_tm": x.reshape(nb * t // P, P, c),
        "f_cm": f.transpose(0, 2, 1).reshape(nb * cb, P, t),
        "cond": np.asarray(cond_512),
        "w": np.asarray(L0_cond_w).reshape(cb, P).T,
        "u": np.asarray(L0_cond_u).reshape(cb, P).T,
        "weights": np.concatenate([first, second], axis=1),
        "bias": np.asarray(L0_ffn_bias),
        "rb1": np.asarray(L0_ffn_rb1),
        "rw2": np.asarray(L0_ffn_rw2)[:e].T,
        "rb2": np.asarray(L0_ffn_rb2)[:e],
        "gates": np.asarray(L0_ffn_gates),
        "ident": np.eye(P, dtype=np.float32),
        "iota": np.arange(e, dtype=np.float32),
    }
    arrays = {name: np.ascontiguousarray(a) for name, a in arrays.items()}
    nc = bacc.Bacc("TRN2", target_bir_lowering=False, num_devices=1, dynamic_dma_scratch_size=1024)
    args = [nc.dram_tensor(name, a.shape, mybir.dt.from_np(a.dtype), kind="ExternalInput").ap()
            for name, a in arrays.items()]
    out = nc.dram_tensor("out", (nb * t // P, P, c), mybir.dt.float32, kind="ExternalOutput").ap()
    bidirectional_decay_mix_with_routed_lora(nc, *args, out)
    result = run_bass_kernel_spmd(nc, [arrays], core_ids=[0])
    return result.results[0]["out"].reshape(nb, t, c)
```
